# Optimizing a Trainium2 kernel written in Bass

```python
import numpy as np
import jax
import jax.numpy as jnp

def _softmax(x, axis=-1):
    return jax.nn.softmax(x, axis=axis)

def _gelu(x):
    return jax.nn.gelu(x, approximate=True)

def _silu(x):
    return jax.nn.silu(x)

def _sigmoid(x):
    return jax.nn.sigmoid(x)

def _layernorm(x, axis=-1, eps=1e-05):
    m = jnp.mean(x, axis=axis, keepdims=True)
    v = jnp.var(x, axis=axis, keepdims=True)
    return (x - m) / jnp.sqrt(v + eps)

def _scatter_add(tgt, idx, src, axis=0):
    return tgt.at[idx].add(src)

def _segment_sum(src, seg, n):
    return jax.ops.segment_sum(src, seg, n)
kernel_name = 'mk_adaln_d1_jaxref_r4_1663d6'

def setup_inputs(seed: int=0):
    np.random.seed(seed)
    _w = jnp.asarray

    def _L0_attn_setup():
        import jax, jax.numpy as jnp
        import numpy as np
        B, L, H = (1, 512, 512)
        E, N, K, R = (1024, 16, 4, 128)

        def _mamba_mixer(hidden_states, in_proj_w, conv_w, conv_b, x_proj_w, dt_proj_w, dt_proj_b, A_log, D, out_proj_w):
            proj = jnp.einsum('blh,eh->ble', hidden_states, in_proj_w)
            h, gate = jnp.split(proj, 2, axis=-1)
            h_c = h.transpose(0, 2, 1)
            h_c = jax.lax.conv_general_dilated(h_c, conv_w, window_strides=(1,), padding=[(K - 1, 0)], feature_group_count=E, dimension_numbers=('NCH', 'OIH', 'NCH'))
            h_c = h_c + conv_b[None, :, None]
            h = jax.nn.silu(h_c).transpose(0, 2, 1)
            ssm = jnp.einsum('ble,pe->blp', h, x_proj_w)
            dt, Bp, Cp = jnp.split(ssm, [R, R + N], axis=-1)
            dt = jax.nn.softplus(jnp.einsum('blr,er->ble', dt, dt_proj_w) + dt_proj_b)
            A = -jnp.exp(A_log)
            dA = jnp.exp(dt[..., None] * A)
            dBu = (dt * h)[..., None] * Bp[:, :, None, :]

            def step(s, xs):
                dA_t, dBu_t = xs
                s = s * dA_t + dBu_t
                return (s, s)
            s0 = jnp.zeros((h.shape[0], E, N), h.dtype)
            _, states = jax.lax.scan(step, s0, (dA.transpose(1, 0, 2, 3), dBu.transpose(1, 0, 2, 3)))
            y = jnp.einsum('lben,bln->ble', states, Cp)
            y = y + h * D
            y = y * jax.nn.silu(gate)
            return jnp.einsum('ble,he->blh', y, out_proj_w)
        key = jax.random.key(seed)
        ks = jax.random.split(key, 8)
        s = 0.02
        inp = {'hidden_states': jax.random.normal(ks[0], (B, L, H), jnp.float32), 'in_proj_w': jax.random.normal(ks[1], (2 * E, H), jnp.float32) * s, 'conv_w': jax.random.normal(ks[2], (E, 1, K), jnp.float32) * s, 'conv_b': jax.random.normal(ks[3], (E,), jnp.float32) * s, 'x_proj_w': jax.random.normal(ks[4], (R + 2 * N, E), jnp.float32) * s, 'dt_proj_w': jax.random.normal(ks[5], (E, R), jnp.float32) * s, 'dt_proj_b': jax.random.normal(ks[6], (E,), jnp.float32) * s, 'A_log': jnp.broadcast_to(jnp.log(jnp.arange(1, N + 1, dtype=jnp.float32))[None, :], (E, N)).copy(), 'D': jnp.ones((E,), jnp.float32), 'out_proj_w': jax.random.normal(ks[7], (H, E), jnp.float32) * s}
        return inp
    _L0_attn_in = _L0_attn_setup()

    def _L0_ffn_setup():
        import math
        import jax, jax.numpy as jnp
        import numpy as np
        DIM = 512
        RANK = 8
        B, T = (4, 1024)

        def _orthogonal(key, n):
            a = jax.random.normal(key, (n, n), dtype=jnp.float32)
            q, r = jnp.linalg.qr(a)
            q = q * jnp.sign(jnp.diagonal(r))[None, :]
            return q
        key = jax.random.key(seed)
        kx, kf = jax.random.split(key)
        x = jax.random.normal(kx, (B, T, DIM), dtype=jnp.float32)
        fkeys = jax.random.split(kf, RANK)
        factors = jnp.stack([_orthogonal(fkeys[r], DIM) * (r + 1) ** (-0.5) for r in range(RANK)])
        bias = jnp.zeros((DIM,), dtype=jnp.float32)
        return {'x': x, 'factors': factors, 'bias': bias}
    _L0_ffn_in = _L0_ffn_setup()
    _L0_c = _w((lambda *s: np.random.randn(*s).astype(np.float32) * 0.05)(2, 512))
    _L0_wmod = _w((lambda *s: np.random.randn(*s).astype(np.float32) * 0.05)(512, 6 * 512) * 512 ** (-0.5))
    _d = {'L0_attn_hidden_states': _L0_attn_in['hidden_states'], 'L0_attn_in_proj_w': _L0_attn_in['in_proj_w'], 'L0_attn_conv_w': _L0_attn_in['conv_w'], 'L0_attn_conv_b': _L0_attn_in['conv_b'], 'L0_attn_x_proj_w': _L0_attn_in['x_proj_w'], 'L0_attn_dt_proj_w': _L0_attn_in['dt_proj_w'], 'L0_attn_dt_proj_b': _L0_attn_in['dt_proj_b'], 'L0_attn_A_log': _L0_attn_in['A_log'], 'L0_attn_D': _L0_attn_in['D'], 'L0_attn_out_proj_w': _L0_attn_in['out_proj_w'], 'L0_ffn_factors': _L0_ffn_in['factors'], 'L0_ffn_bias': _L0_ffn_in['bias'], 'L0_c': _L0_c, 'L0_wmod': _L0_wmod}
    _x0 = _d['L0_attn_hidden_states']
    _d['L0_attn_hidden_states'] = jax.random.normal(jax.random.fold_in(jax.random.key(seed), 1), (2, 2048, 512), dtype=_x0.dtype)
    del _x0
    return _d

def reference(L0_attn_hidden_states, L0_attn_in_proj_w, L0_attn_conv_w, L0_attn_conv_b, L0_attn_x_proj_w, L0_attn_dt_proj_w, L0_attn_dt_proj_b, L0_attn_A_log, L0_attn_D, L0_attn_out_proj_w, L0_ffn_factors, L0_ffn_bias, L0_c, L0_wmod):

    def _L0_attn_ref(hidden_states, in_proj_w, conv_w, conv_b, x_proj_w, dt_proj_w, dt_proj_b, A_log, D, out_proj_w):
        import jax, jax.numpy as jnp
        import numpy as np
        B, L, H = (1, 512, 512)
        E, N, K, R = (1024, 16, 4, 128)

        def _mamba_mixer(hidden_states, in_proj_w, conv_w, conv_b, x_proj_w, dt_proj_w, dt_proj_b, A_log, D, out_proj_w):
            proj = jnp.einsum('blh,eh->ble', hidden_states, in_proj_w)
            h, gate = jnp.split(proj, 2, axis=-1)
            h_c = h.transpose(0, 2, 1)
            h_c = jax.lax.conv_general_dilated(h_c, conv_w, window_strides=(1,), padding=[(K - 1, 0)], feature_group_count=E, dimension_numbers=('NCH', 'OIH', 'NCH'))
            h_c = h_c + conv_b[None, :, None]
            h = jax.nn.silu(h_c).transpose(0, 2, 1)
            ssm = jnp.einsum('ble,pe->blp', h, x_proj_w)
            dt, Bp, Cp = jnp.split(ssm, [R, R + N], axis=-1)
            dt = jax.nn.softplus(jnp.einsum('blr,er->ble', dt, dt_proj_w) + dt_proj_b)
            A = -jnp.exp(A_log)
            dA = jnp.exp(dt[..., None] * A)
            dBu = (dt * h)[..., None] * Bp[:, :, None, :]

            def step(s, xs):
                dA_t, dBu_t = xs
                s = s * dA_t + dBu_t
                return (s, s)
            s0 = jnp.zeros((h.shape[0], E, N), h.dtype)
            _, states = jax.lax.scan(step, s0, (dA.transpose(1, 0, 2, 3), dBu.transpose(1, 0, 2, 3)))
            y = jnp.einsum('lben,bln->ble', states, Cp)
            y = y + h * D
            y = y * jax.nn.silu(gate)
            return jnp.einsum('ble,he->blh', y, out_proj_w)
        return _mamba_mixer(hidden_states, in_proj_w, conv_w, conv_b, x_proj_w, dt_proj_w, dt_proj_b, A_log, D, out_proj_w)

    def _L0_ffn_ref(x, factors, bias):
        import math
        import jax, jax.numpy as jnp
        import numpy as np
        DIM = 512
        RANK = 8
        B, T = (4, 1024)

        def _orthogonal(key, n):
            a = jax.random.normal(key, (n, n), dtype=jnp.float32)
            q, r = jnp.linalg.qr(a)
            q = q * jnp.sign(jnp.diagonal(r))[None, :]
            return q
        rank = factors.shape[0]
        mixed = jnp.einsum('btd,rde->bte', x, factors)
        mixed = mixed / math.sqrt(rank) + bias
        return mixed
    x = L0_attn_hidden_states
    mod = (_silu(L0_c) @ L0_wmod).reshape(L0_c.shape[0], 6, 1, -1)
    sa, ca, ga, sb, cb, gb = (mod[:, 0], mod[:, 1], mod[:, 2], mod[:, 3], mod[:, 4], mod[:, 5])
    ga = (2 * (ga >= 0) - 1) * jnp.maximum(jnp.abs(ga), 0.25)
    gb = (2 * (gb >= 0) - 1) * jnp.maximum(jnp.abs(gb), 0.25)
    h = _layernorm(x, axis=-1) * (1 + ca) + sa
    x = x + ga * _L0_attn_ref(h, L0_attn_in_proj_w, L0_attn_conv_w, L0_attn_conv_b, L0_attn_x_proj_w, L0_attn_dt_proj_w, L0_attn_dt_proj_b, L0_attn_A_log, L0_attn_D, L0_attn_out_proj_w)
    h = _layernorm(x, axis=-1) * (1 + cb) + sb
    x = x + gb * _L0_ffn_ref(h, L0_ffn_factors, L0_ffn_bias)
    return x

_drawn_inputs = setup_inputs


def setup_inputs(seed=0):
    import zlib

    import numpy as np

    out = dict(_drawn_inputs(seed))
    spreads = {'L0_attn_D': (1.0, 0.2), 'L0_ffn_bias': (0.0, 0.1)}
    factors = {}
    for name, (base, spread) in spreads.items():
        noise = np.random.default_rng([zlib.crc32(name.encode()), seed]).standard_normal(out[name].shape)
        drawn = base * np.exp(spread * noise) if base else spread * noise
        out[name] = jnp.asarray(drawn.astype(out[name].dtype))
    for name, factor in factors.items():
        out[name] = (out[name] * factor).astype(out[name].dtype)
    return out
```

```python
from contextlib import ExitStack
import math

import concourse.bass as bass
from concourse import mybir

F32 = mybir.dt.float32
ALU = mybir.AluOpType
ACT = mybir.ActivationFunctionType

P = 128
BATCH, SEQ, DIM = 2, 2048, 512
E, N, TAPS, RANK_DT = 1024, 16, 4, 128
RANK = 8
EPS = 1e-5
ROWS = 256
LB = ROWS // P
CHUNKS = BATCH * SEQ // ROWS
KD = DIM // P
KE = E // P
PAIRS = KE // 2
UNITS = N * PAIRS
STEPS = UNITS // 2
HALF = E // 2
RING = 4
CONV_B, DT_B, SKIP, A_AT = TAPS, TAPS + 1, TAPS + 2, TAPS + 3
CHAN = A_AT + N
SA, CA, SB, CB = range(4)
STAGED = [0, 1, 2, 5, 3, 4] + list(range(1, RANK))
MODS = 6
A_JOBS, C_JOBS = 8, 7


def wait(eng, sem, value):
    if not (isinstance(value, int) and value <= 0):
        eng.wait_ge(sem, value)


def build(nc, x, win_t, xp_t, dt_t, wo_t, chan, cond_t, wmod, factors, bias, out):
    x_rows = x.rearrange("b (n t p) d -> b n p t d", t=LB, p=P)
    out_rows = out.rearrange("b (n t p) d -> b n p t d", t=LB, p=P)
    win_v = win_t.rearrange("(k p) e -> p k e", p=P)
    xp_v = xp_t.rearrange("(k p) r -> p k r", p=P)
    wo_v = wo_t.rearrange("(k p) d -> p k d", p=P)
    wmod_v = wmod.rearrange("(k p) (j d) -> j p k d", p=P, j=MODS)
    fac_v = factors.rearrange("r (k p) d -> r p k d", p=P)
    b_dram = nc.dram_tensor("b_scratch", (2, N * ROWS), F32).ap()

    with ExitStack() as ctx:
        def sb(name, shape):
            return ctx.enter_context(nc.sbuf_tensor(name, shape, F32))

        def bank(name):
            return ctx.enter_context(nc.psum_tensor(name, [P, 512], F32))

        def sem(name):
            return ctx.enter_context(nc.semaphore(name))

        win = sb("win", [P, KD, 2 * E])
        xp = sb("xp", [P, KE, RANK_DT + 2 * N])
        dtw = sb("dtw", [P, E])
        wo = sb("wo", [P, KE, DIM])
        ffn = sb("ffn", [P, KD, DIM])
        ga = sb("ga", [P, BATCH, DIM])
        gb = sb("gb", [P, BATCH, DIM])
        ident = sb("ident", [P, P])
        ch = sb("ch", [P, KE, CHAN])
        conv = sb("conv", [P, KE, TAPS + 1])
        decay_rate = sb("decay_rate", [P, KE, N])
        mods = sb("mods", [P, 4, KD, BATCH])
        cond = sb("cond", [P, KD, BATCH])
        cond_s = sb("cond_s", [P, KD, BATCH])
        cond_h = sb("cond_h", [P, KD, BATCH])
        small = sb("small", [P, 3, LB])
        ones_row = sb("ones_row", [1, P])
        bias_row = sb("bias_row", [1, DIM])
        xa = sb("xa", [P, LB, DIM])
        hT = [sb(f"hT{i}", [P, KD, ROWS]) for i in range(2)]
        pre = [sb(f"pre{i}", [P, 2, TAPS - 1 + ROWS]) for i in range(2)]
        hist = [sb(f"hist{i}", [P, KE, TAPS - 1]) for i in range(BATCH)]
        tanh_h = sb("tanh_h", [P, 512])
        hc = sb("hc", [P, KE, ROWS])
        dtr = sb("dtr", [P, ROWS])
        b_s = sb("b_s", [N, ROWS])
        stat_a = sb("stat_a", [P, LB, 6])
        mv_a = sb("mv_a", [P, LB, 2])
        nrm_a = sb("nrm_a", [P, 4, LB])
        dt = [sb(f"dt{i}", [P, KE, ROWS]) for i in range(2)]
        u = [sb(f"u{i}", [P, KE, ROWS]) for i in range(2)]
        b_all = sb("b_all", [P, N, ROWS])
        c_rows = [sb(f"c_rows{i}", [P, LB, N]) for i in range(2)]
        ub = sb("ub", [P, RING, 2, ROWS])
        state = sb("state", [P, RING, 2, ROWS])
        carry = [sb(f"carry{i}", [P, N, KE]) for i in range(BATCH)]
        acc = [sb(f"acc{i}", [P, LB, E]) for i in range(2)]
        xc = sb("xc", [P, LB, DIM])
        tanh_g = sb("tanh_g", [P, 512])
        yg = sb("yg", [P, KE, ROWS])
        z2 = sb("z2", [P, LB, DIM])
        h2T = xa[:, :, :].rearrange("p t d -> p (t d)").rearrange("p (k r) -> p k r", k=KD)
        stat_c = sb("stat_c", [P, LB, 6])
        mv_c = sb("mv_c", [P, LB, 2])
        nrm_c = sb("nrm_c", [P, 4, LB])
        staged = [acc[1][:, :, :].rearrange("p t e -> p (t e)").rearrange("p (k d) -> p k d", k=KD),
                  yg[:, :, :].rearrange("p k r -> p (k r)").rearrange("p (k d) -> p k d", k=KD)]
        cond_all = z2[:, :, :].rearrange("p t d -> p (t d)").rearrange("p (k b q) -> p k b q", k=KD, b=BATCH)

        decay = [bank(f"decay{i}") for i in range(2)]
        turn = [bank(f"turn{i}") for i in range(LB)]
        bank_a = [bank(f"bank_a{i}") for i in range(2)]
        bank_c = [bank(f"bank_c{i}") for i in range(2)]

        ub_made, decay_made, scanned, turned = sem("ub_made"), sem("decay_made"), sem("scanned"), sem("turned")
        summed, carried = sem("summed"), sem("carried")
        a_full = [sem(f"a_full{i}") for i in range(2)]
        a_free = [sem(f"a_free{i}") for i in range(2)]
        c_full = [sem(f"c_full{i}") for i in range(2)]
        c_free = [sem(f"c_free{i}") for i in range(2)]
        xa_loaded, bn_a, stats_a, norm_a, z_a = sem("xa_loaded"), sem("bn_a"), sem("stats_a"), sem("norm_a"), sem("z_a")
        pre_made, tap_done, tanh_h_made, skip_made = sem("pre_made"), sem("tap_done"), sem("tanh_h_made"), sem("skip_made")
        soft_exp, soft_ln, dt_made, u_made = sem("soft_exp"), sem("soft_ln"), sem("dt_made"), sem("u_made")
        b_stored, h_copied = sem("b_stored"), sem("h_copied")
        b_loaded = [sem(f"b_loaded{i}") for i in range(2)]
        xc_loaded, bn_c, stats_c, norm_c, z_c = sem("xc_loaded"), sem("bn_c"), sem("stats_c"), sem("norm_c"), sem("z_c")
        tanh_g_made, o_scaled, f_scaled, out_stored = sem("tanh_g_made"), sem("o_scaled"), sem("f_scaled"), sem("out_stored")
        small_loaded, win_h_loaded, xp_loaded, late_loaded = sem("small_loaded"), sem("win_h_loaded"), sem("xp_loaded"), sem("late_loaded")
        stage_loaded = [sem(f"stage_loaded{i}") for i in range(2)]
        stage_used = [sem(f"stage_used{i}") for i in range(2)]
        consts_made, rate_exp, cond_tanh, prep = sem("consts_made"), sem("rate_exp"), sem("cond_tanh"), sem("prep")
        mods_made, rows_abs, rows_sign, rows_made, ident_set = sem("mods_made"), sem("rows_abs"), sem("rows_sign"), sem("rows_made"), sem("ident_set")

        block = ctx.enter_context(nc.Block())

        def rounds(eng, one_round):
            one_round(0, 0, 0, None)
            with eng.Fori(0, CHUNKS // 2 - 1) as i:
                one_round(2 * i + 1, 1, i + 1, i)
                one_round(2 * i + 2, 0, i + 1, i)
            one_round(CHUNKS - 1, 1, None, CHUNKS // 2 - 1)

        @block.sync
        def _(sp):
            def load_stage(j):
                src = wmod_v[STAGED[j]] if j < MODS else fac_v[STAGED[j]]
                if j >= 2:
                    sp.wait_ge(stage_used[j % 2], j // 2)
                if j == 3:
                    sp.wait_ge(a_full[0], A_JOBS)
                    sp.wait_ge(a_full[1], A_JOBS)
                sp.dma_start(staged[j % 2], src).then_inc(stage_loaded[j % 2], 16)

            def store_b(c, par):
                sp.wait_ge(a_free[0], A_JOBS * c + 4)
                sp.dma_start(b_dram[par].rearrange("(n r) -> n r", n=N), b_s[:, :]).then_inc(b_stored, 16)

            def load_b(c, par, h):
                wait(sp, ub_made, UNITS * (c - 1) + (h + 1) * UNITS // 2)
                sp.wait_ge(b_stored, 16 * c + 16)
                n0 = h * N // 2
                src = b_dram[par:par + 1, n0 * ROWS:(n0 + N // 2) * ROWS].to_broadcast([P, N * ROWS // 2])
                sp.dma_start(b_all[:, n0:n0 + N // 2, :].rearrange("p n r -> p (n r)"), src).then_inc(b_loaded[h], 16)

            sp.dma_start(ch[:, :, :], chan).then_inc(small_loaded, 16)
            sp.dma_start(cond[:, :, :], cond_t).then_inc(small_loaded, 16)
            sp.dma_start(xa[:, :, :], x_rows[0, 0]).then_inc(xa_loaded, 16)
            load_stage(0)
            load_stage(1)
            sp.dma_start(win[:, :, 0:E], win_v[:, :, 0:E]).then_inc(win_h_loaded, 16)
            sp.dma_start(xp[:, :, :], xp_v).then_inc(xp_loaded, 16)
            sp.dma_start(dtw[:, :], dt_t).then_inc(xp_loaded, 16)
            sp.dma_start(win[:, :, E:2 * E], win_v[:, :, E:2 * E]).then_inc(late_loaded, 16)
            sp.dma_start(wo[:, :, :], wo_v).then_inc(late_loaded, 16)
            sp.dma_start(ffn[:, :, :], fac_v[0]).then_inc(late_loaded, 16)
            sp.dma_start(bias_row[:, :], bias.rearrange("(a d) -> a d", a=1)).then_inc(late_loaded, 16)
            store_b(0, 0)
            load_b(0, 0, 0)

            def one_round(c, par, la, lc):
                if lc is not None:
                    sp.wait_ge(rows_made, 2 * BATCH)
                    wait(sp, out_stored, 16 * (c - 1))
                    sp.dma_start(xc[:, :, :], x_rows[1 - par, lc]).then_inc(xc_loaded, 16)
                if la is not None:
                    sp.wait_ge(a_full[1], A_JOBS * c + 1)
                    sp.wait_ge(a_full[0], A_JOBS * c + 1)
                    sp.dma_start(xa[:, :, :], x_rows[1 - par, la]).then_inc(xa_loaded, 16)
                load_b(c, par, 1)
                if isinstance(c, int) and c == 0:
                    for j in range(2, len(STAGED)):
                        load_stage(j)
                if lc is not None:
                    store_out(c - 1, 1 - par, lc)
                if la is not None:
                    store_b(c + 1, 1 - par)
                    load_b(c + 1, 1 - par, 0)

            def store_out(c, par, lc):
                sp.wait_ge(c_free[0], C_JOBS * c + C_JOBS)
                sp.wait_ge(c_free[1], C_JOBS * c + C_JOBS)
                sp.dma_start(out_rows[par, lc], xc[:, :, :]).then_inc(out_stored, 16)

            rounds(sp, one_round)
            last = CHUNKS - 1
            sp.wait_ge(out_stored, 16 * last)
            sp.dma_start(xc[:, :, :], x_rows[1, CHUNKS // 2 - 1]).then_inc(xc_loaded, 16)
            store_out(last, 1, CHUNKS // 2 - 1)
            sp.wait_ge(out_stored, 16 * CHUNKS)
            sp.wait_ge(b_stored, 16 * CHUNKS)

        @block.gpsimd
        def _(pool):
            pool.memset(ident[:, :], 1.0).then_inc(ident_set, 1)
            pool.wait_ge(ident_set, 1)
            pool.affine_select(out=ident[:, :], in_=ident[:, :], compare_op=ALU.is_equal, fill=0.0, base=0,
                               pattern=[[-1, P]], channel_multiplier=1).then_inc(consts_made, 1)
            for i, value in enumerate((-0.5, EPS, -1.0)):
                last = pool.memset(small[:, i, :], value)
            last.then_inc(ident_set, 1)
            for b in range(BATCH):
                pool.memset(carry[b][:, :, :], 0.0)
                last = pool.memset(hist[b][:, :, :], 0.0)
            last.then_inc(consts_made, 1)
            pool.memset(ones_row[:, :], 1.0).then_inc(consts_made, 1)
            pool.wait_ge(ident_set, 2)

            def norm(c, mv, nrm, stats, chain, used):
                pool.wait_ge(stats, c + 1)
                wait(pool, used, c)
                pool.tensor_tensor(nrm[:, 0, :], mv[:, :, 1], small[:, 1, :], ALU.add).then_inc(chain, 1)
                pool.tensor_tensor(nrm[:, 1, :], mv[:, :, 0], small[:, 2, :], ALU.mult).then_inc(chain, 1)
                pool.wait_ge(chain, 4 * c + 2)
                pool.tensor_tensor(nrm[:, 2, :], nrm[:, 0, :], small[:, 0, :], ALU.pow).then_inc(chain, 1)
                pool.wait_ge(chain, 4 * c + 3)
                pool.tensor_tensor(nrm[:, 3, :], nrm[:, 1, :], nrm[:, 2, :], ALU.mult).then_inc(chain, 1)

            def norm_before(c):
                norm(c, mv_a, nrm_a, stats_a, norm_a, z_a)

            def norm_after(c):
                norm(c, mv_c, nrm_c, stats_c, norm_c, z_c)

            def make_dt_u(c, par, h):
                k = slice(h * KE // 2, (h + 1) * KE // 2)
                pool.wait_ge(soft_ln, c + 1)
                pool.tensor_tensor(dt[par][:, k, :], dt[par][:, k, :], u[par][:, k, :], ALU.add).then_inc(dt_made, 1)
                pool.wait_ge(dt_made, 2 * c + h + 1)
                pool.tensor_tensor(u[par][:, k, :], dt[par][:, k, :], hc[:, k, :], ALU.mult).then_inc(u_made, 1)

            def make_ub(c, par, g):
                n, q = g // PAIRS, g % PAIRS
                if g == 0:
                    pool.wait_ge(u_made, 2 * c + 2)
                if g % (UNITS // 2) == 0:
                    pool.wait_ge(b_loaded[g // (UNITS // 2)], 16 * c + 16)
                wait(pool, scanned, UNITS * c + g - RING + 1)
                pool.tensor_tensor(ub[:, g % RING, :, :], u[par][:, 2 * q:2 * q + 2, :],
                                   b_all[:, n:n + 1, :].to_broadcast([P, 2, ROWS]), ALU.mult).then_inc(ub_made, 1)

            norm_before(0)
            make_dt_u(0, 0, 0)
            make_dt_u(0, 0, 1)

            def one_round(c, par, la, lc):
                for s in range(STEPS):
                    make_ub(c, par, 2 * s)
                    make_ub(c, par, 2 * s + 1)
                    if la is not None:
                        if s == 4:
                            norm_before(c + 1)
                        if s in (29, 30):
                            make_dt_u(c + 1, 1 - par, s - 29)
                    if lc is not None and s == 14:
                        norm_after(c - 1)

            rounds(pool, one_round)
            norm_after(CHUNKS - 1)

        @block.scalar
        def _(act):
            def decays(c, par, g):
                n, q = g // PAIRS, g % PAIRS
                if g == 0:
                    act.wait_ge(dt_made, 2 * c + 2)
                wait(act, scanned, UNITS * c + g - 1)
                for j in range(2):
                    e = 2 * q + j
                    last = act.activation(decay[g % 2][:, j * ROWS:(j + 1) * ROWS], dt[par][:, e, :], ACT.Exp,
                                          scale=decay_rate[:, e, n:n + 1])
                last.then_inc(decay_made, 1)

            def keep_carry(c, par, s):
                n, eh, slot = s // 2, s % 2, 2 * (s % 2)
                act.wait_ge(scanned, UNITS * c + 2 * s + 2)
                act.activation(carry[par][:, n, 4 * eh:4 * eh + 4].rearrange("p (a j) -> p a j", a=2),
                               state[:, slot:slot + 2, :, ROWS - 1], ACT.Copy).then_inc(carried, 1)

            def normalize(c, nrm, src, dst, chain, done):
                act.wait_ge(chain, 4 * c + 4)
                for t in range(LB):
                    last = act.activation(dst[:, t, :], src[:, t, :], ACT.Identity,
                                          bias=nrm[:, 3, t:t + 1], scale=nrm[:, 2, t:t + 1])
                last.then_inc(done, 1)

            def modulate(src, dst, j, b, shift, scale):
                for i in range(2):
                    k = 2 * j + i
                    last = act.activation(dst[:, k, :], src[:, i * ROWS:(i + 1) * ROWS], ACT.Identity,
                                          bias=mods[:, shift, k, b:b + 1], scale=mods[:, scale, k, b:b + 1])
                return last

            def z_before(c):
                normalize(c, nrm_a, xa, xa, norm_a, z_a)

            def modulate_before(c, par, j):
                act.wait_ge(a_full[j], A_JOBS * c + 1)
                if not isinstance(c, int) or c >= 2:
                    act.wait_ge(c_full[1], C_JOBS * (c - 2) + 2)
                modulate(bank_a[j], hT[par], j, par, SA, CA).then_inc(a_free[j], 1)

            def copy_h(c, par, q):
                i, bk = q % 2, bank_a[q % 2]
                h = bk[:, :].rearrange("p (j r) -> p j r", j=2)
                pair = slice(2 * q, 2 * q + 2)
                act.wait_ge(a_full[i], A_JOBS * c + 2 + q // 2)
                wait(act, tap_done, 6 * (4 * c + q - 1))
                step = 3 * (PAIRS * c + q)
                act.activation(pre[i][:, :, 0:TAPS - 1], hist[par][:, pair, :], ACT.Copy).then_inc(h_copied, 1)
                act.activation(pre[i][:, :, TAPS - 1:], h, ACT.Copy).then_inc(h_copied, 1)
                act.wait_ge(h_copied, step + 1)
                act.activation(hist[par][:, pair, :], h[:, :, ROWS - TAPS + 1:], ACT.Copy).then_inc(h_copied, 1)
                act.wait_ge(h_copied, step + 3)
                for j in range(2):
                    e = 2 * q + j
                    last = act.activation(h[:, j, :], h[:, j, :], ACT.Identity,
                                          bias=conv[:, e, TAPS:TAPS + 1], scale=conv[:, e, TAPS - 1:TAPS])
                last.then_inc(pre_made, 1)

            def tanh_before(c, q):
                act.wait_ge(tap_done, 6 * (4 * c + q + 1))
                if q:
                    act.wait_ge(a_free[(q - 1) % 2], A_JOBS * c + 2 + (q - 1) // 2)
                act.activation(tanh_h[:, :], bank_a[q % 2][:, :], ACT.Tanh).then_inc(tanh_h_made, 1)

            def skip(c, q):
                act.wait_ge(a_free[q % 2], A_JOBS * c + 2 + q // 2)
                if not isinstance(c, int) or c >= 2:
                    act.wait_ge(c_full[1], C_JOBS * (c - 2) + 5)
                if isinstance(c, int) and c == 1:
                    act.wait_ge(stage_used[1], len(STAGED) // 2)
                for e in (2 * q, 2 * q + 1):
                    last = act.activation(yg[:, e, :], hc[:, e, :], ACT.Identity, scale=ch[:, e, SKIP:SKIP + 1])
                last.then_inc(skip_made, 1)

            def copy_dt_b(c):
                act.wait_ge(a_full[0], A_JOBS * c + 4)
                act.activation(dtr[:, :], bank_a[0][:, 0:ROWS], ACT.Copy)
                wait(act, b_stored, 16 * c)
                act.activation(b_s[:, :], bank_a[0][0:N, ROWS:2 * ROWS], ACT.Copy).then_inc(a_free[0], 1)

            def copy_c(c, par):
                act.wait_ge(a_full[1], A_JOBS * c + 4)
                if not isinstance(c, int) or c >= 2:
                    act.wait_ge(summed, STEPS * (c - 1))
                act.activation(c_rows[par][:, :, :].rearrange("p t n -> p (t n)"), bank_a[1][:, 0:LB * N],
                               ACT.Copy).then_inc(a_free[1], 1)

            def split_dt(c, par, q):
                act.wait_ge(a_full[q % 2], A_JOBS * c + 5 + q // 2)
                if not isinstance(c, int) or c >= 2:
                    act.wait_ge(ub_made, UNITS * (c - 1))
                for j in range(2):
                    e, src = 2 * q + j, bank_a[q % 2][:, j * ROWS:(j + 1) * ROWS]
                    act.activation(dt[par][:, e, :], src, ACT.Relu, bias=ch[:, e, DT_B:DT_B + 1])
                    last = act.activation(u[par][:, e, :], src, ACT.Abs, bias=ch[:, e, DT_B:DT_B + 1])
                last.then_inc(a_free[q % 2], 1)

            def softplus(c, par):
                act.wait_ge(a_free[0], A_JOBS * c + 6)
                act.wait_ge(a_free[1], A_JOBS * c + 6)
                act.activation(u[par][:, :, :], u[par][:, :, :], ACT.Exp, scale=-1.0).then_inc(soft_exp, 1)
                act.wait_ge(soft_exp, c + 1)
                act.activation(u[par][:, :, :], u[par][:, :, :], ACT.Ln, bias=1.0).then_inc(soft_ln, 1)

            def start_acc(c, par, j):
                t, eh = j // 2, j % 2
                act.wait_ge(a_full[j % 2], A_JOBS * c + 7 + j // 2)
                if isinstance(c, int) and c == 1:
                    act.wait_ge(stage_used[0], (len(STAGED) + 1) // 2)
                act.activation(acc[par][:, t, eh * HALF:(eh + 1) * HALF], bank_a[j % 2][:, :],
                               ACT.Copy).then_inc(a_free[j % 2], 1)

            def tanh_gate(c, q):
                act.wait_ge(c_full[q % 2], C_JOBS * c + q // 2 + 1)
                if q:
                    act.wait_ge(c_free[(q - 1) % 2], C_JOBS * c + (q - 1) // 2 + 1)
                act.activation(tanh_g[:, :], bank_c[q % 2][:, :], ACT.Tanh, scale=0.5).then_inc(tanh_g_made, 1)

            def z_after(c):
                normalize(c, nrm_c, xc, z2, norm_c, z_c)

            def modulate_after(c, par, j):
                act.wait_ge(c_full[j], C_JOBS * c + 6)
                if j == 0 and not (isinstance(c, int) and c >= CHUNKS - 2):
                    act.wait_ge(a_full[0], A_JOBS * (c + 2) + 1)
                    act.wait_ge(a_full[1], A_JOBS * (c + 2) + 1)
                modulate(bank_c[j], h2T, j, par, SB, CB).then_inc(c_free[j], 1)

            def rows_absolute(i):
                act.wait_ge(stage_used[i], 2)
                wait(act, rows_made, BATCH * i)
                for b in range(BATCH):
                    last = act.activation(xc[:, b, :], bank_c[b][:, :], ACT.Abs)
                last.then_inc(rows_abs, 1)

            act.wait_ge(small_loaded, 32)
            act.activation(decay_rate[:, :, :], ch[:, :, A_AT:], ACT.Exp).then_inc(rate_exp, 1)
            act.activation(cond_s[:, :, :], cond[:, :, :], ACT.Tanh, scale=0.5).then_inc(cond_tanh, 1)

            z_before(0)
            act.wait_ge(mods_made, 2)
            act.wait_ge(prep, 3)
            act.wait_ge(consts_made, 3)
            modulate_before(0, 0, 0)
            modulate_before(0, 0, 1)
            for q in range(PAIRS):
                copy_h(0, 0, q)
                tanh_before(0, q)
            for q in range(PAIRS):
                skip(0, q)
            copy_dt_b(0)
            copy_c(0, 0)
            for q in range(PAIRS):
                split_dt(0, 0, q)
            softplus(0, 0)
            for j in range(2 * LB):
                start_acc(0, 0, j)
            act.wait_ge(prep, 5)

            def one_round(c, par, la, lc):
                first = isinstance(c, int) and c == 0
                for s in range(STEPS):
                    decays(c, par, 2 * s)
                    decays(c, par, 2 * s + 1)
                    if s:
                        keep_carry(c, par, s - 1)
                    elif not first:
                        keep_carry(c - 1, 1 - par, STEPS - 1)
                    if first and s in (1, 3):
                        rows_absolute(s // 2)
                    if lc is not None:
                        if 1 <= s <= 4:
                            tanh_gate(c - 1, s - 1)
                        if s == 14:
                            z_after(c - 1)
                        if s == 16:
                            act.wait_ge(mods_made, 4)
                            modulate_after(c - 1, 1 - par, 0)
                            modulate_after(c - 1, 1 - par, 1)
                    if la is not None:
                        if s == 4:
                            z_before(c + 1)
                        if s == 6:
                            modulate_before(c + 1, 1 - par, 0)
                            modulate_before(c + 1, 1 - par, 1)
                        if s in (7, 8, 13, 14):
                            copy_h(c + 1, 1 - par, {7: 0, 8: 1, 13: 2, 14: 3}[s])
                        if s in (9, 10, 15, 16):
                            tanh_before(c + 1, {9: 0, 10: 1, 15: 2, 16: 3}[s])
                        if 17 <= s <= 20:
                            skip(c + 1, s - 17)
                        if s == 22:
                            copy_dt_b(c + 1)
                            copy_c(c + 1, 1 - par)
                        if s == 24:
                            split_dt(c + 1, 1 - par, 0)
                            split_dt(c + 1, 1 - par, 1)
                        if s == 26:
                            split_dt(c + 1, 1 - par, 2)
                            split_dt(c + 1, 1 - par, 3)
                            softplus(c + 1, 1 - par)
                        if s == 28:
                            start_acc(c + 1, 1 - par, 0)
                            start_acc(c + 1, 1 - par, 1)
                        if s == 29:
                            start_acc(c + 1, 1 - par, 2)
                            start_acc(c + 1, 1 - par, 3)

            rounds(act, one_round)
            last = CHUNKS - 1
            for q in range(PAIRS):
                tanh_gate(last, q)
            z_after(last)
            modulate_after(last, 1, 0)
            modulate_after(last, 1, 1)

        @block.tensor
        def _(pe):
            def turn_states(c, g):
                s, q = g // 2, g % 2
                pe.wait_ge(scanned, UNITS * c + g + 1)
                if q == 0:
                    wait(pe, summed, STEPS * c + s)
                for j in range(2):
                    for t in range(LB):
                        at = (2 * q + j) * P
                        last = pe.transpose(turn[t][:, at:at + P], state[:, g % RING, j, t * P:(t + 1) * P], ident[:, :])
                last.then_inc(turned, 1)

            def turn_x(c, j):
                pe.wait_ge(z_a, c + 1)
                wait(pe, a_free[j], A_JOBS * c)
                for i in range(2):
                    for t in range(LB):
                        k = 2 * j + i
                        last = pe.transpose(bank_a[j][:, i * ROWS + t * P:i * ROWS + (t + 1) * P],
                                            xa[:, t, k * P:(k + 1) * P], ident[:, :])
                last.then_inc(a_full[j], 1)

            def project_in(dst, full, hTc, m0, q):
                for j in range(2):
                    m = m0 + 2 * q + j
                    for k in range(KD):
                        last = pe.matmul(dst[:, j * ROWS:(j + 1) * ROWS], win[:, k, m * P:(m + 1) * P], hTc[:, k, :],
                                         start=(k == 0), stop=(k == KD - 1))
                last.then_inc(full, 1)

            def project_h(c, par, q):
                pe.wait_ge(a_free[q % 2], A_JOBS * c + 1 + q // 2)
                if q == 0:
                    pe.wait_ge(a_free[1], A_JOBS * c + 1)
                project_in(bank_a[q % 2], a_full[q % 2], hT[par], 0, q)

            def project_dt(c):
                pe.wait_ge(a_free[0], A_JOBS * c + 3)
                pe.wait_ge(a_free[1], A_JOBS * c + 3)
                for k in range(KE):
                    pe.matmul(bank_a[0][:, 0:ROWS], xp[:, k, 0:RANK_DT], hc[:, k, :], start=(k == 0), stop=(k == KE - 1))

            def project_b(c):
                for k in range(KE):
                    last = pe.matmul(bank_a[0][0:N, ROWS:2 * ROWS], xp[:, k, RANK_DT:RANK_DT + N], hc[:, k, :],
                                     start=(k == 0), stop=(k == KE - 1))
                last.then_inc(a_full[0], 1)

            def project_c(c):
                for t in range(LB):
                    for k in range(KE):
                        last = pe.matmul(bank_a[1][:, t * N:(t + 1) * N], hc[:, k, t * P:(t + 1) * P],
                                         xp[:, k, RANK_DT + N:], start=(k == 0), stop=(k == KE - 1))
                last.then_inc(a_full[1], 1)

            def expand_dt(c, q):
                if q == 0:
                    pe.wait_ge(a_free[0], A_JOBS * c + 4)
                pe.wait_ge(a_free[q % 2], A_JOBS * c + 4 + q // 2)
                for j in range(2):
                    m = 2 * q + j
                    last = pe.matmul(bank_a[q % 2][:, j * ROWS:(j + 1) * ROWS], dtw[:, m * P:(m + 1) * P], dtr[:, :],
                                     start=True, stop=True)
                last.then_inc(a_full[q % 2], 1)

            def turn_skip(c, j):
                t, eh = j // 2, j % 2
                pe.wait_ge(skip_made, PAIRS * (c + 1))
                pe.wait_ge(a_free[j % 2], A_JOBS * c + 6 + j // 2)
                for i in range(4):
                    last = pe.transpose(bank_a[j % 2][:, i * P:(i + 1) * P], yg[:, 4 * eh + i, t * P:(t + 1) * P],
                                        ident[:, :])
                last.then_inc(a_full[j % 2], 1)

            def project_gate(c, par, q):
                wait(pe, c_free[q % 2], C_JOBS * c + q // 2)
                project_in(bank_c[q % 2], c_full[q % 2], hT[par], KE, q)

            def turn_sums(c, par, q):
                if q == 0:
                    pe.wait_ge(summed, STEPS * (c + 1))
                pe.wait_ge(c_free[q % 2], C_JOBS * c + 2 + q // 2)
                for j in range(2):
                    for t in range(LB):
                        m = 2 * q + j
                        last = pe.transpose(bank_c[q % 2][:, j * ROWS + t * P:j * ROWS + (t + 1) * P],
                                            acc[par][:, t, m * P:(m + 1) * P], ident[:, :])
                last.then_inc(c_full[q % 2], 1)

            def project_out(c, t, h):
                pe.wait_ge(c_free[0], C_JOBS * c + 4)
                pe.wait_ge(c_free[1], C_JOBS * c + (4 if t or h else 3))
                for k in range(h * KE // 2, (h + 1) * KE // 2):
                    last = pe.matmul(bank_c[t][:, :], yg[:, k, t * P:(t + 1) * P], wo[:, k, :],
                                     start=(k == 0), stop=(k == KE - 1))
                if h:
                    last.then_inc(c_full[t], 1)

            def turn_z(c, j):
                pe.wait_ge(z_c, c + 1)
                pe.wait_ge(c_free[j], C_JOBS * c + 5)
                for i in range(2):
                    for t in range(LB):
                        k = 2 * j + i
                        last = pe.transpose(bank_c[j][:, i * ROWS + t * P:i * ROWS + (t + 1) * P],
                                            z2[:, t, k * P:(k + 1) * P], ident[:, :])
                last.then_inc(c_full[j], 1)

            def project_ffn(c, t):
                pe.wait_ge(c_free[0], C_JOBS * c + 6)
                pe.wait_ge(c_free[1], C_JOBS * c + 6)
                pe.matmul(bank_c[t][:, :], ones_row[:, :], bias_row[:, :], start=True, stop=False)
                for k in range(KD):
                    last = pe.matmul(bank_c[t][:, :], h2T[:, k, t * P:(t + 1) * P], ffn[:, k, :],
                                     start=False, stop=(k == KD - 1))
                last.then_inc(c_full[t], 1)

            def mod_columns(j):
                pe.wait_ge(stage_loaded[j % 2], 16 * (j // 2 + 1))
                if j in (1, 5):
                    pe.wait_ge(mods_made, j // 4 * 2 + 1)
                if j == 4:
                    pe.wait_ge(rows_made, 2 * BATCH)
                for m in range(KD):
                    for k in range(KD):
                        last = pe.matmul(bank_c[0][:, m * BATCH:(m + 1) * BATCH], staged[j % 2][:, k, m * P:(m + 1) * P],
                                         cond_h[:, k, :], start=(k == 0), stop=(k == KD - 1))
                last.then_inc(stage_used[j % 2], 1)

            def mod_rows(j):
                pe.wait_ge(stage_loaded[j % 2], 16 * (j // 2 + 1))
                if j == 2:
                    pe.wait_ge(mods_made, 2)
                    pe.wait_ge(prep, 6)
                wait(pe, rows_made, BATCH * (j - 2))
                for b in range(BATCH):
                    for k in range(KD):
                        last = pe.matmul(bank_c[b][:, :], cond_all[:, k, b, :], staged[j % 2][:, k, :],
                                         start=(k == 0), stop=(k == KD - 1))
                last.then_inc(stage_used[j % 2], 1)

            pe.wait_ge(prep, 2)
            mod_columns(0)
            mod_columns(1)
            pe.wait_ge(consts_made, 3)
            turn_x(0, 0)
            turn_x(0, 1)
            pe.wait_ge(win_h_loaded, 16)
            for q in range(PAIRS):
                project_h(0, 0, q)
            pe.wait_ge(xp_loaded, 32)
            project_dt(0)
            project_b(0)
            project_c(0)
            for q in range(PAIRS):
                expand_dt(0, q)
            for j in range(2 * LB):
                turn_skip(0, j)

            def one_round(c, par, la, lc):
                first = isinstance(c, int) and c == 0
                for s in range(STEPS):
                    turn_states(c, 2 * s)
                    turn_states(c, 2 * s + 1)
                    if first:
                        if s in (0, 2):
                            mod_rows(2 + s // 2)
                        if s in (4, 5):
                            mod_columns(s)
                        if s == STEPS - 1:
                            pe.wait_ge(late_loaded, 64)
                    if lc is not None:
                        if s < 4:
                            if s == 0:
                                pe.wait_ge(mods_made, 4)
                                pe.wait_ge(prep, 7)
                                pe.wait_ge(stage_used[0], (len(STAGED) + 1) // 2)
                            project_gate(c - 1, 1 - par, s)
                        elif s < 8:
                            turn_sums(c - 1, 1 - par, s - 4)
                        elif s < 12:
                            project_out(c - 1, (s - 8) // 2, s % 2)
                        if s == 15:
                            turn_z(c - 1, 0)
                            turn_z(c - 1, 1)
                        if s in (17, 18):
                            project_ffn(c - 1, s - 17)
                    if la is not None:
                        if s == 5:
                            turn_x(c + 1, 0)
                            turn_x(c + 1, 1)
                        if s in (6, 7, 12, 13):
                            project_h(c + 1, 1 - par, {6: 0, 7: 1, 12: 2, 13: 3}[s])
                        if s == 19:
                            project_dt(c + 1)
                        if s == 20:
                            project_b(c + 1)
                        if s == 21:
                            project_c(c + 1)
                        if s == 23:
                            expand_dt(c + 1, 0)
                            expand_dt(c + 1, 1)
                        if s == 25:
                            expand_dt(c + 1, 2)
                            expand_dt(c + 1, 3)
                        if s == 27:
                            turn_skip(c + 1, 0)
                            turn_skip(c + 1, 1)
                        if s == 28:
                            turn_skip(c + 1, 2)
                            turn_skip(c + 1, 3)

            rounds(pe, one_round)
            last = CHUNKS - 1
            for q in range(PAIRS):
                project_gate(last, 1, q)
            for q in range(PAIRS):
                turn_sums(last, 1, q)
            for t in range(LB):
                for h in range(2):
                    project_out(last, t, h)
            turn_z(last, 0)
            turn_z(last, 1)
            project_ffn(last, 0)
            project_ffn(last, 1)

        @block.vector
        def _(dve):
            def scan(c, par, g):
                n, q = g // PAIRS, g % PAIRS
                dve.wait_ge(decay_made, UNITS * c + g + 1)
                dve.wait_ge(ub_made, UNITS * c + g + 1)
                wait(dve, turned, UNITS * c + g - RING + 1)
                wait(dve, carried, STEPS * c + (g - RING) // 2 + 1)
                for j in range(2):
                    last = dve.tensor_tensor_scan(state[:, g % RING, j, :], decay[g % 2][:, j * ROWS:(j + 1) * ROWS],
                                                  ub[:, g % RING, j, :], carry[par][:, n, 2 * q + j:2 * q + j + 1],
                                                  ALU.mult, ALU.add)
                last.then_inc(scanned, 1)

            def add_states(c, par, s):
                n, eh = s // 2, s % 2
                if s == 0:
                    dve.wait_ge(a_free[0], A_JOBS * (c + 1))
                    dve.wait_ge(a_free[1], A_JOBS * (c + 1))
                dve.wait_ge(turned, UNITS * c + 2 * s + 2)
                wait(dve, summed, STEPS * c + s - 1)
                for t in range(LB):
                    part = acc[par][:, t, eh * HALF:(eh + 1) * HALF]
                    last = dve.scalar_tensor_tensor(out=part, in0=turn[t][:, :], scalar=c_rows[par][:, t, n:n + 1],
                                                    in1=part, op0=ALU.mult, op1=ALU.add)
                last.then_inc(summed, 1)

            def stats(c, src, stat, bn, used):
                wait(dve, used, 4 * c)
                for t in range(LB):
                    last = dve.bn_stats(stat[:, t, :], src[:, t, :])
                last.then_inc(bn, 1)

            def means(stat, mv, done):
                for t in range(LB):
                    last = dve.bn_aggr(mv[:, t, :], stat[:, t, :])
                last.then_inc(done, 1)

            def stats_before(c):
                dve.wait_ge(xa_loaded, 16 * c + 16)
                stats(c, xa, stat_a, bn_a, norm_a)

            def taps(c, q):
                bk = bank_a[q % 2]
                dve.wait_ge(pre_made, PAIRS * c + q + 1)
                for k in range(TAPS - 1):
                    for j in range(2):
                        e, part = 2 * q + j, bk[:, j * ROWS:(j + 1) * ROWS]
                        if k:
                            dve.wait_ge(tap_done, 6 * (4 * c + q) + 2 * (k - 1) + j + 1)
                        dve.scalar_tensor_tensor(out=part, in0=pre[q % 2][:, j, k:k + ROWS], scalar=conv[:, e, k:k + 1],
                                                 in1=part, op0=ALU.mult, op1=ALU.add).then_inc(tap_done, 1)

            def silu_before(c, q):
                dve.wait_ge(tanh_h_made, PAIRS * c + q + 1)
                if q == 0:
                    wait(dve, u_made, 2 * c)
                    wait(dve, skip_made, PAIRS * c)
                dve.scalar_tensor_tensor(out=hc[:, 2 * q:2 * q + 2, :].rearrange("p k r -> p (k r)"), in0=tanh_h[:, :],
                                         scalar=1.0, in1=bank_a[q % 2][:, :], op0=ALU.add,
                                         op1=ALU.mult).then_inc(a_free[q % 2], 1)

            def silu_gate(c, q):
                if q == 0:
                    done = min(c + 2, CHUNKS) if isinstance(c, int) else c + 2
                    dve.wait_ge(a_full[0], A_JOBS * done)
                    dve.wait_ge(a_full[1], A_JOBS * done)
                dve.wait_ge(tanh_g_made, PAIRS * c + q + 1)
                dve.scalar_tensor_tensor(out=yg[:, 2 * q:2 * q + 2, :].rearrange("p k r -> p (k r)"), in0=tanh_g[:, :],
                                         scalar=1.0, in1=bank_c[q % 2][:, :], op0=ALU.add,
                                         op1=ALU.mult).then_inc(c_free[q % 2], 1)

            def gate_sums(c, q):
                dve.wait_ge(c_full[q % 2], C_JOBS * c + 3 + q // 2)
                part = yg[:, 2 * q:2 * q + 2, :].rearrange("p k r -> p (k r)")
                dve.tensor_tensor(part, bank_c[q % 2][:, :], part, ALU.mult).then_inc(c_free[q % 2], 1)

            def residual(c, t, job, gates, par, chain):
                dve.wait_ge(c_full[t], C_JOBS * c + job)
                dve.tensor_tensor(bank_c[t][:, :], bank_c[t][:, :], gates[:, par, :], ALU.mult).then_inc(chain, 1)
                dve.wait_ge(chain, LB * c + t + 1)
                dve.tensor_tensor(xc[:, t, :], bank_c[t][:, :], xc[:, t, :], ALU.add).then_inc(c_free[t], 1)

            def residual_mixer(c, par, t):
                if t == 0:
                    dve.wait_ge(xc_loaded, 16 * c + 16)
                residual(c, t, 5, ga, par, o_scaled)

            def stats_after(c):
                dve.wait_ge(c_free[0], C_JOBS * c + 5)
                dve.wait_ge(c_free[1], C_JOBS * c + 5)
                stats(c, xc, stat_c, bn_c, norm_c)

            def residual_ffn(c, par, t):
                residual(c, t, 7, gb, par, f_scaled)

            def copy_mods(j, kind):
                dve.wait_ge(stage_used[j % 2], j // 2 + 1)
                dst = mods[:, kind, :, :].rearrange("p k b -> p (k b)")
                one = 1.0 if kind in (CA, CB) else 0.0
                dve.tensor_scalar(dst, bank_c[0][:, 0:KD * BATCH], one, None, ALU.add).then_inc(mods_made, 1)

            def clamp_rows(i, gates, factor):
                dve.wait_ge(rows_abs, i + 1)
                for b in range(BATCH):
                    n = 2 * BATCH * i + 2 * b
                    g = gates[:, b, :]
                    dve.tensor_scalar(g, bank_c[b][:, :], 0.0, 2.0 * factor, ALU.is_ge, ALU.mult).then_inc(rows_sign, 1)
                    dve.wait_ge(rows_sign, n + 1)
                    dve.tensor_scalar(g, g, -factor, None, ALU.add).then_inc(rows_sign, 1)
                    dve.wait_ge(rows_sign, n + 2)
                    dve.scalar_tensor_tensor(out=g, in0=xc[:, b, :], scalar=0.25, in1=g, op0=ALU.max,
                                             op1=ALU.mult).then_inc(rows_made, 1)

            def add_factor(j):
                dve.wait_ge(stage_loaded[j % 2], 16 * (j // 2 + 1))
                if j > MODS:
                    dve.wait_ge(stage_used[(j - 1) % 2], (j - 1) // 2 + 1)
                dve.tensor_tensor(ffn[:, :, :], ffn[:, :, :], staged[j % 2], ALU.add).then_inc(stage_used[j % 2], 1)

            dve.wait_ge(cond_tanh, 1)
            dve.scalar_tensor_tensor(out=cond_s[:, :, :], in0=cond_s[:, :, :], scalar=1.0, in1=cond[:, :, :],
                                     op0=ALU.add, op1=ALU.mult).then_inc(prep, 1)
            dve.wait_ge(prep, 1)
            dve.tensor_scalar(cond_h[:, :, :], cond_s[:, :, :], 0.5, None, ALU.mult).then_inc(prep, 1)
            dve.tensor_scalar(conv[:, :, :], ch[:, :, 0:TAPS + 1], 0.5, None, ALU.mult).then_inc(prep, 1)
            stats_before(0)
            dve.wait_ge(bn_a, 1)
            means(stat_a, mv_a, stats_a)
            copy_mods(0, SA)
            copy_mods(1, CA)
            dve.wait_ge(prep, 2)
            dve.tensor_copy(cond_all, cond_h[:, :, :].unsqueeze(3).to_broadcast([P, KD, BATCH, P])).then_inc(prep, 1)
            dve.wait_ge(rate_exp, 1)
            dve.tensor_scalar(decay_rate[:, :, :], decay_rate[:, :, :], -1.0, None, ALU.mult).then_inc(prep, 1)
            dve.wait_ge(late_loaded, 64)
            dve.tensor_scalar(bias_row[:, :], bias_row[:, :], math.sqrt(RANK), None, ALU.mult).then_inc(prep, 2)
            for q in range(PAIRS):
                taps(0, q)
                silu_before(0, q)

            def one_round(c, par, la, lc):
                first = isinstance(c, int) and c == 0
                for s in range(STEPS):
                    if la is not None and s == 3:
                        dve.wait_ge(bn_a, c + 2)
                    if lc is not None and s == 13:
                        dve.wait_ge(bn_c, c)
                    scan(c, par, 2 * s)
                    if la is not None and s == 3:
                        means(stat_a, mv_a, stats_a)
                    if lc is not None and s == 13:
                        means(stat_c, mv_c, stats_c)
                    if s:
                        add_states(c, par, s - 1)
                    elif not first:
                        add_states(c - 1, 1 - par, STEPS - 1)
                    scan(c, par, 2 * s + 1)
                    if first:
                        if s in (1, 3):
                            clamp_rows(s // 2, *[(ga, 0.5), (gb, RANK ** -0.5)][s // 2])
                        if s in (5, 6):
                            copy_mods(s - 1, (SB, CB)[s - 5])
                        if MODS < s < MODS + RANK:
                            add_factor(s - 1)
                    if lc is not None:
                        if 1 <= s <= 4:
                            silu_gate(c - 1, s - 1)
                        elif 5 <= s <= 8:
                            gate_sums(c - 1, s - 5)
                        if s in (10, 12):
                            residual_mixer(c - 1, 1 - par, s // 2 - 5)
                        if s == 12:
                            stats_after(c - 1)
                        if s in (19, 20):
                            residual_ffn(c - 1, 1 - par, s - 19)
                    if la is not None:
                        if s == 2:
                            stats_before(c + 1)
                        if s in (7, 8, 13, 14):
                            taps(c + 1, {7: 0, 8: 1, 13: 2, 14: 3}[s])
                        if s in (9, 10, 15, 16):
                            silu_before(c + 1, {9: 0, 10: 1, 15: 2, 16: 3}[s])

            rounds(dve, one_round)
            last = CHUNKS - 1
            add_states(last, 1, STEPS - 1)
            for q in range(PAIRS):
                silu_gate(last, q)
            for q in range(PAIRS):
                gate_sums(last, q)
            residual_mixer(last, 1, 0)
            residual_mixer(last, 1, 1)
            stats_after(last)
            dve.wait_ge(bn_c, CHUNKS)
            means(stat_c, mv_c, stats_c)
            residual_ffn(last, 1, 0)
            residual_ffn(last, 1, 1)


def kernel(**inputs):
    import numpy as np
    import concourse.bacc as bacc
    from concourse.bass_utils import run_bass_kernel_spmd

    def tiles(a):
        a = np.asarray(a)
        return a.reshape(a.shape[0] // P, P, -1).transpose(1, 0, 2)

    at = {k.removeprefix("L0_"): np.asarray(v) for k, v in inputs.items()}
    chan = np.concatenate([tiles(at[k]) for k in ("attn_conv_w", "attn_conv_b", "attn_dt_proj_b", "attn_D", "attn_A_log")], axis=2)
    arrays = {
        "x": at["attn_hidden_states"], "win_t": at["attn_in_proj_w"].T, "xp_t": at["attn_x_proj_w"].T,
        "dt_t": at["attn_dt_proj_w"].T, "wo_t": at["attn_out_proj_w"].T, "chan": chan,
        "cond_t": tiles(at["c"].T), "wmod": at["wmod"], "factors": at["ffn_factors"], "bias": at["ffn_bias"],
    }
    arrays = {k: np.ascontiguousarray(v) for k, v in arrays.items()}
    nc = bacc.Bacc("TRN2", target_bir_lowering=False, num_devices=1)
    args = [nc.dram_tensor(k, v.shape, mybir.dt.from_np(v.dtype), kind="ExternalInput").ap() for k, v in arrays.items()]
    out = nc.dram_tensor("out", (BATCH, SEQ, DIM), F32, kind="ExternalOutput").ap()
    build(nc, *args, out)
    r = run_bass_kernel_spmd(nc, [arrays], core_ids=[0])
    return r.results[0]["out"]
```

```python
from contextlib import ExitStack
import math

import concourse.bass as bass
from concourse import mybir

F32 = mybir.dt.float32
ALU = mybir.AluOpType
ACT = mybir.ActivationFunctionType

P = 128
BATCH, SEQ, DIM = 2, 2048, 512
E, N, TAPS, RANK_DT = 1024, 16, 4, 128
RANK = 8
EPS = 1e-5
ROWS = 256
LB = ROWS // P
CHUNKS = BATCH * SEQ // ROWS
KD = DIM // P
KE = E // P
PAIRS = KE // 2
UNITS = N * PAIRS
STEPS = UNITS // 2
HALF = E // 2
RING = 4
CONV_B, DT_B, SKIP, A_AT = TAPS, TAPS + 1, TAPS + 2, TAPS + 3
CHAN = A_AT + N
SA, CA, SB, CB = range(4)
STAGED = [0, 1, 2, 5, 3, 4] + list(range(1, RANK))
MODS = 6
A_JOBS, C_JOBS = 8, 7


def wait(eng, sem, value):
    if not (isinstance(value, int) and value <= 0):
        eng.wait_ge(sem, value)


def build(nc, x, win_t, xp_t, dt_t, wo_t, chan, cond_t, wmod, factors, bias, out):
    x_rows = x.rearrange("b (n t p) d -> b n p t d", t=LB, p=P)
    out_rows = out.rearrange("b (n t p) d -> b n p t d", t=LB, p=P)
    win_v = win_t.rearrange("(k p) e -> p k e", p=P)
    xp_v = xp_t.rearrange("(k p) r -> p k r", p=P)
    wo_v = wo_t.rearrange("(k p) d -> p k d", p=P)
    wmod_v = wmod.rearrange("(k p) (j d) -> j p k d", p=P, j=MODS)
    fac_v = factors.rearrange("r (k p) d -> r p k d", p=P)
    b_dram = nc.dram_tensor("b_scratch", (2, N * ROWS), F32).ap()

    with ExitStack() as ctx:
        def sb(name, shape):
            return ctx.enter_context(nc.sbuf_tensor(name, shape, F32))

        def bank(name):
            return ctx.enter_context(nc.psum_tensor(name, [P, 512], F32))

        def sem(name):
            return ctx.enter_context(nc.semaphore(name))

        win = sb("win", [P, KD, 2 * E])
        xp = sb("xp", [P, KE, RANK_DT + 2 * N])
        dtw = sb("dtw", [P, E])
        wo = sb("wo", [P, KE, DIM])
        ffn = sb("ffn", [P, KD, DIM])
        ga = sb("ga", [P, BATCH, DIM])
        gb = sb("gb", [P, BATCH, DIM])
        ident = sb("ident", [P, P])
        ch = sb("ch", [P, KE, CHAN])
        conv = sb("conv", [P, KE, TAPS + 1])
        decay_rate = sb("decay_rate", [P, KE, N])
        mods = sb("mods", [P, 4, KD, BATCH])
        cond = sb("cond", [P, KD, BATCH])
        cond_s = sb("cond_s", [P, KD, BATCH])
        cond_h = sb("cond_h", [P, KD, BATCH])
        small = sb("small", [P, 3, LB])
        ones_row = sb("ones_row", [1, P])
        bias_row = sb("bias_row", [1, DIM])
        xa = sb("xa", [P, LB, DIM])
        hT = [sb(f"hT{i}", [P, KD, ROWS]) for i in range(2)]
        pre = [sb(f"pre{i}", [P, 2, TAPS - 1 + ROWS]) for i in range(2)]
        hist = [sb(f"hist{i}", [P, KE, TAPS - 1]) for i in range(BATCH)]
        tanh_h = sb("tanh_h", [P, 512])
        hc = sb("hc", [P, KE, ROWS])
        dtr = sb("dtr", [P, ROWS])
        b_s = sb("b_s", [N, ROWS])
        stat_a = sb("stat_a", [P, LB, 6])
        mv_a = sb("mv_a", [P, LB, 2])
        nrm_a = sb("nrm_a", [P, 4, LB])
        dt = [sb(f"dt{i}", [P, KE, ROWS]) for i in range(2)]
        u = [sb(f"u{i}", [P, KE, ROWS]) for i in range(2)]
        b_all = sb("b_all", [P, N, ROWS])
        c_rows = [sb(f"c_rows{i}", [P, LB, N]) for i in range(2)]
        ub = sb("ub", [P, RING, 2, ROWS])
        state = sb("state", [P, RING, 2, ROWS])
        carry = [sb(f"carry{i}", [P, N, KE]) for i in range(BATCH)]
        seam = [sb(f"seam{i}", [P, N, PAIRS]) for i in range(2)]
        acc = [sb(f"acc{i}", [P, LB, E]) for i in range(2)]
        xc = sb("xc", [P, LB, DIM])
        tanh_g = sb("tanh_g", [P, 512])
        yg = sb("yg", [P, KE, ROWS])
        z2 = sb("z2", [P, LB, DIM])
        h2T = xa[:, :, :].rearrange("p t d -> p (t d)").rearrange("p (k r) -> p k r", k=KD)
        stat_c = sb("stat_c", [P, LB, 6])
        mv_c = sb("mv_c", [P, LB, 2])
        nrm_c = sb("nrm_c", [P, 4, LB])
        staged = [acc[1][:, :, :].rearrange("p t e -> p (t e)").rearrange("p (k d) -> p k d", k=KD),
                  yg[:, :, :].rearrange("p k r -> p (k r)").rearrange("p (k d) -> p k d", k=KD)]
        cond_all = z2[:, :, :].rearrange("p t d -> p (t d)").rearrange("p (k b q) -> p k b q", k=KD, b=BATCH)

        decay = [bank(f"decay{i}") for i in range(2)]
        turn = [bank(f"turn{i}") for i in range(LB)]
        bank_a = [bank(f"bank_a{i}") for i in range(2)]
        bank_c = [bank(f"bank_c{i}") for i in range(2)]

        ub_made, decay_made, scanned, turned = sem("ub_made"), sem("decay_made"), sem("scanned"), sem("turned")
        summed, carried = sem("summed"), sem("carried")
        ub_product, seam_decay, seam_made, seam_zeroed = sem("ub_product"), sem("seam_decay"), sem("seam_made"), sem("seam_zeroed")
        a_full = [sem(f"a_full{i}") for i in range(2)]
        a_free = [sem(f"a_free{i}") for i in range(2)]
        c_full = [sem(f"c_full{i}") for i in range(2)]
        c_free = [sem(f"c_free{i}") for i in range(2)]
        xa_loaded, bn_a, stats_a, norm_a, z_a = sem("xa_loaded"), sem("bn_a"), sem("stats_a"), sem("norm_a"), sem("z_a")
        pre_made, tap_done, tanh_h_made, skip_made = sem("pre_made"), sem("tap_done"), sem("tanh_h_made"), sem("skip_made")
        soft_exp, soft_ln, dt_made, u_made = sem("soft_exp"), sem("soft_ln"), sem("dt_made"), sem("u_made")
        b_stored, h_copied = sem("b_stored"), sem("h_copied")
        b_loaded = [sem(f"b_loaded{i}") for i in range(2)]
        xc_loaded, bn_c, stats_c, norm_c, z_c = sem("xc_loaded"), sem("bn_c"), sem("stats_c"), sem("norm_c"), sem("z_c")
        tanh_g_made, o_scaled, f_scaled, out_stored = sem("tanh_g_made"), sem("o_scaled"), sem("f_scaled"), sem("out_stored")
        small_loaded, win_h_loaded, xp_loaded, late_loaded = sem("small_loaded"), sem("win_h_loaded"), sem("xp_loaded"), sem("late_loaded")
        stage_loaded = [sem(f"stage_loaded{i}") for i in range(2)]
        stage_used = [sem(f"stage_used{i}") for i in range(2)]
        consts_made, rate_exp, cond_tanh, prep = sem("consts_made"), sem("rate_exp"), sem("cond_tanh"), sem("prep")
        bias_scaled = sem("bias_scaled")
        mods_made, rows_abs, rows_sign, rows_made, ident_set = sem("mods_made"), sem("rows_abs"), sem("rows_sign"), sem("rows_made"), sem("ident_set")

        block = ctx.enter_context(nc.Block())

        def rounds(eng, one_round):
            one_round(0, 0, 0, None)
            with eng.Fori(0, CHUNKS // 2 - 1) as i:
                one_round(2 * i + 1, 1, i + 1, i)
                one_round(2 * i + 2, 0, i + 1, i)
            one_round(CHUNKS - 1, 1, None, CHUNKS // 2 - 1)

        @block.sync
        def _(sp):
            def load_stage(j):
                src = wmod_v[STAGED[j]] if j < MODS else fac_v[STAGED[j]]
                if j >= 2:
                    sp.wait_ge(stage_used[j % 2], j // 2)
                if j == 3:
                    sp.wait_ge(a_full[0], A_JOBS)
                    sp.wait_ge(a_full[1], A_JOBS)
                sp.dma_start(staged[j % 2], src).then_inc(stage_loaded[j % 2], 16)

            def store_b(c, par):
                sp.wait_ge(a_free[1], A_JOBS * c + 4)
                sp.dma_start(b_dram[par].rearrange("(n r) -> n r", n=N), b_s[:, :]).then_inc(b_stored, 16)

            def load_b(c, par, h):
                wait(sp, ub_made, STEPS * (c - 1) + (h + 1) * STEPS // 2)
                sp.wait_ge(b_stored, 16 * c + 16)
                n0 = h * N // 2
                src = b_dram[par:par + 1, n0 * ROWS:(n0 + N // 2) * ROWS].to_broadcast([P, N * ROWS // 2])
                sp.dma_start(b_all[:, n0:n0 + N // 2, :].rearrange("p n r -> p (n r)"), src).then_inc(b_loaded[h], 16)

            sp.dma_start(ch[:, :, :], chan).then_inc(small_loaded, 16)
            sp.dma_start(cond[:, :, :], cond_t).then_inc(small_loaded, 16)
            sp.dma_start(xa[:, :, :], x_rows[0, 0]).then_inc(xa_loaded, 16)
            load_stage(0)
            load_stage(1)
            sp.dma_start(win[:, :, 0:E], win_v[:, :, 0:E]).then_inc(win_h_loaded, 16)
            sp.dma_start(xp[:, :, :], xp_v).then_inc(xp_loaded, 16)
            sp.dma_start(dtw[:, :], dt_t).then_inc(xp_loaded, 16)
            sp.dma_start(win[:, :, E:2 * E], win_v[:, :, E:2 * E]).then_inc(late_loaded, 16)
            sp.dma_start(wo[:, :, :], wo_v).then_inc(late_loaded, 16)
            sp.dma_start(ffn[:, :, :], fac_v[0]).then_inc(late_loaded, 16)
            sp.dma_start(bias_row[:, :], bias.rearrange("(a d) -> a d", a=1)).then_inc(late_loaded, 16)
            store_b(0, 0)
            load_b(0, 0, 0)

            def one_round(c, par, la, lc):
                if la is not None:
                    sp.wait_ge(xa_loaded, 16)
                    if isinstance(c, int) and c == 0:
                        sp.wait_ge(a_full[1], 1)
                        sp.wait_ge(a_full[0], 1)
                    else:
                        sp.wait_ge(c_full[0], C_JOBS * (c - 1) + 1)
                    sp.dma_start(xa[:, :, :], x_rows[1 - par, la]).then_inc(xa_loaded, 16)
                if lc is not None:
                    sp.wait_ge(rows_made, 2 * BATCH)
                    wait(sp, out_stored, 16 * (c - 1))
                    sp.dma_start(xc[:, :, :], x_rows[1 - par, lc]).then_inc(xc_loaded, 16)
                load_b(c, par, 1)
                if isinstance(c, int) and c == 0:
                    for j in range(2, len(STAGED)):
                        load_stage(j)
                if la is not None:
                    store_b(c + 1, 1 - par)
                    load_b(c + 1, 1 - par, 0)
                if lc is not None:
                    store_out(c - 1, 1 - par, lc)

            def store_out(c, par, lc):
                sp.wait_ge(c_free[0], C_JOBS * c + C_JOBS)
                sp.wait_ge(c_free[1], C_JOBS * c + C_JOBS)
                sp.dma_start(out_rows[par, lc], xc[:, :, :]).then_inc(out_stored, 16)

            rounds(sp, one_round)
            last = CHUNKS - 1
            sp.wait_ge(out_stored, 16 * last)
            sp.dma_start(xc[:, :, :], x_rows[1, CHUNKS // 2 - 1]).then_inc(xc_loaded, 16)
            store_out(last, 1, CHUNKS // 2 - 1)
            sp.wait_ge(out_stored, 16 * CHUNKS)
            sp.wait_ge(b_stored, 16 * CHUNKS)

        @block.gpsimd
        def _(pool):
            pool.memset(ident[:, :], 1.0).then_inc(ident_set, 1)
            pool.wait_ge(ident_set, 1)
            pool.affine_select(out=ident[:, :], in_=ident[:, :], compare_op=ALU.is_equal, fill=0.0, base=0,
                               pattern=[[-1, P]], channel_multiplier=1).then_inc(consts_made, 1)
            for i, value in enumerate((-0.5, EPS, -1.0)):
                last = pool.memset(small[:, i, :], value)
            last.then_inc(ident_set, 1)
            for b in range(BATCH):
                pool.memset(carry[b][:, :, :], 0.0)
                last = pool.memset(hist[b][:, :, :], 0.0)
            last.then_inc(consts_made, 1)
            pool.memset(ones_row[:, :], 1.0).then_inc(consts_made, 1)
            pool.wait_ge(ident_set, 2)

            def norm(c, mv, nrm, stats, chain, used):
                pool.wait_ge(stats, c + 1)
                wait(pool, used, c)
                pool.tensor_tensor(nrm[:, 0, :], mv[:, :, 1], small[:, 1, :], ALU.add).then_inc(chain, 1)
                pool.tensor_tensor(nrm[:, 1, :], mv[:, :, 0], small[:, 2, :], ALU.mult).then_inc(chain, 1)
                pool.wait_ge(chain, 4 * c + 2)
                pool.tensor_tensor(nrm[:, 2, :], nrm[:, 0, :], small[:, 0, :], ALU.pow).then_inc(chain, 1)
                pool.wait_ge(chain, 4 * c + 3)
                pool.tensor_tensor(nrm[:, 3, :], nrm[:, 1, :], nrm[:, 2, :], ALU.mult).then_inc(chain, 1)

            def norm_before(c):
                norm(c, mv_a, nrm_a, stats_a, norm_a, z_a)

            def norm_after(c):
                norm(c, mv_c, nrm_c, stats_c, norm_c, z_c)

            def make_u(c, par, h):
                k = slice(h * KE // 2, (h + 1) * KE // 2)
                pool.wait_ge(dt_made, 2 * c + h + 1)
                pool.tensor_tensor(u[par][:, k, :], dt[par][:, k, :], hc[:, k, :], ALU.mult).then_inc(u_made, 1)

            def make_seam(c, par):
                pool.wait_ge(seam_decay, c + 1)
                wait(pool, carried, STEPS * (c - 1))
                odd = carry[par][:, :, :].rearrange("p n (q j) -> p n q j", j=2)[:, :, :, 1]
                pool.tensor_tensor(seam[par][:, :, :], seam[par][:, :, :], odd, ALU.mult).then_inc(seam_made, 1)

            def make_ub(c, par, s):
                n, q, slot = s // 2, 2 * (s % 2), 2 * (s % 2)
                if s == 0:
                    pool.wait_ge(u_made, 2 * c + 2)
                if s % (STEPS // 2) == 0:
                    pool.wait_ge(b_loaded[s // (STEPS // 2)], 16 * c + 16)
                wait(pool, scanned, UNITS * c + 2 * s - RING + 2)
                product = ub[:, slot:slot + 2, :, :].rearrange("p g j r -> p (g j) r")
                pool.tensor_tensor(product, u[par][:, 2 * q:2 * q + 4, :],
                                   b_all[:, n:n + 1, :].to_broadcast([P, 4, ROWS]), ALU.mult).then_inc(ub_product, 1)
                if s == 0:
                    make_seam(c, par)
                    pool.wait_ge(seam_made, c + 1)
                pool.wait_ge(ub_product, STEPS * c + s + 1)
                first = ub[:, slot:slot + 2, 1, 0]
                pool.tensor_tensor(first, first, seam[par][:, n, q:q + 2], ALU.add).then_inc(ub_made, 1)

            norm_before(0)
            make_u(0, 0, 0)
            make_u(0, 0, 1)

            def one_round(c, par, la, lc):
                for s in range(STEPS):
                    make_ub(c, par, s)
                    if la is not None:
                        if s == 4:
                            norm_before(c + 1)
                        if s in (29, 30):
                            make_u(c + 1, 1 - par, s - 29)
                    if lc is not None and s == 19:
                        norm_after(c - 1)

            rounds(pool, one_round)
            norm_after(CHUNKS - 1)

        @block.scalar
        def _(act):
            def decays(c, par, g):
                n, q = g // PAIRS, g % PAIRS
                if g == 0:
                    act.wait_ge(dt_made, 2 * c + 2)
                wait(act, scanned, UNITS * c + g - 1)
                for j in range(2):
                    e = 2 * q + j
                    last = act.activation(decay[g % 2][:, j * ROWS + j:(j + 1) * ROWS], dt[par][:, e, j:], ACT.Exp,
                                          scale=decay_rate[:, e, n:n + 1])
                last.then_inc(decay_made, 1)

            def keep_carry(c, par, s):
                n, eh, slot = s // 2, s % 2, 2 * (s % 2)
                act.wait_ge(scanned, UNITS * c + 2 * s + 2)
                act.activation(carry[par][:, n, 4 * eh:4 * eh + 4].rearrange("p (a j) -> p a j", a=2),
                               state[:, slot:slot + 2, :, ROWS - 1], ACT.Copy).then_inc(carried, 1)

            def normalize(c, nrm, src, dst, chain, done):
                act.wait_ge(chain, 4 * c + 4)
                for t in range(LB):
                    last = act.activation(dst[:, t, :], src[:, t, :], ACT.Identity,
                                          bias=nrm[:, 3, t:t + 1], scale=nrm[:, 2, t:t + 1])
                last.then_inc(done, 1)

            def modulate(src, dst, j, b, shift, scale):
                for i in range(2):
                    k = 2 * j + i
                    last = act.activation(dst[:, k, :], src[:, i * ROWS:(i + 1) * ROWS], ACT.Identity,
                                          bias=mods[:, shift, k, b:b + 1], scale=mods[:, scale, k, b:b + 1])
                return last

            def z_before(c):
                normalize(c, nrm_a, xa, xa, norm_a, z_a)

            def modulate_before(c, par, j):
                act.wait_ge(a_full[j], A_JOBS * c + 1)
                if not isinstance(c, int) or c >= 2:
                    act.wait_ge(c_full[1], C_JOBS * (c - 2) + 2)
                modulate(bank_a[j], hT[par], j, par, SA, CA).then_inc(a_free[j], 1)

            def copy_h(c, par, q):
                i, bk = q % 2, bank_a[q % 2]
                h = bk[:, :].rearrange("p (j r) -> p j r", j=2)
                pair = slice(2 * q, 2 * q + 2)
                act.wait_ge(a_full[i], A_JOBS * c + 2 + q // 2)
                wait(act, tap_done, 6 * (4 * c + q - 1))
                step = 3 * (PAIRS * c + q)
                act.activation(pre[i][:, :, 0:TAPS - 1], hist[par][:, pair, :], ACT.Copy).then_inc(h_copied, 1)
                act.activation(pre[i][:, :, TAPS - 1:], h, ACT.Copy).then_inc(h_copied, 1)
                act.wait_ge(h_copied, step + 1)
                act.activation(hist[par][:, pair, :], h[:, :, ROWS - TAPS + 1:], ACT.Copy).then_inc(h_copied, 1)
                act.wait_ge(h_copied, step + 3)
                for j in range(2):
                    e = 2 * q + j
                    last = act.activation(h[:, j, :], h[:, j, :], ACT.Identity,
                                          bias=conv[:, e, TAPS:TAPS + 1], scale=conv[:, e, TAPS - 1:TAPS])
                last.then_inc(pre_made, 1)

            def tanh_before(c, q):
                act.wait_ge(tap_done, 6 * (4 * c + q + 1))
                if q:
                    act.wait_ge(a_free[(q - 1) % 2], A_JOBS * c + 2 + (q - 1) // 2)
                act.activation(tanh_h[:, :], bank_a[q % 2][:, :], ACT.Tanh).then_inc(tanh_h_made, 1)

            def skip(c, q):
                act.wait_ge(a_free[q % 2], A_JOBS * c + 2 + q // 2)
                if not isinstance(c, int) or c >= 2:
                    act.wait_ge(c_full[1], C_JOBS * (c - 2) + 5)
                if isinstance(c, int) and c == 1:
                    act.wait_ge(stage_used[1], len(STAGED) // 2)
                for e in (2 * q, 2 * q + 1):
                    last = act.activation(yg[:, e, :], hc[:, e, :], ACT.Identity, scale=ch[:, e, SKIP:SKIP + 1])
                last.then_inc(skip_made, 1)

            def copy_dt(c):
                act.wait_ge(a_full[0], A_JOBS * c + 4)
                act.activation(dtr[:, :], bank_a[0][:, 0:ROWS], ACT.Copy).then_inc(a_free[0], 1)

            def copy_b_c(c, par):
                act.wait_ge(a_full[1], A_JOBS * c + 4)
                wait(act, b_stored, 16 * c)
                act.activation(b_s[:, :], bank_a[1][0:N, ROWS:2 * ROWS], ACT.Copy)
                if not isinstance(c, int) or c >= 2:
                    act.wait_ge(summed, STEPS * (c - 1))
                act.activation(c_rows[par][:, :, :].rearrange("p t n -> p (t n)"), bank_a[1][:, 0:LB * N],
                               ACT.Copy).then_inc(a_free[1], 1)

            def split_dt(c, par, q):
                act.wait_ge(a_full[q % 2], A_JOBS * c + 5 + q // 2)
                if not isinstance(c, int) or c >= 2:
                    act.wait_ge(ub_made, STEPS * (c - 1))
                for j in range(2):
                    e, src = 2 * q + j, bank_a[q % 2][:, j * ROWS:(j + 1) * ROWS]
                    act.activation(dt[par][:, e, :], src, ACT.Relu, bias=ch[:, e, DT_B:DT_B + 1])
                    last = act.activation(u[par][:, e, :], src, ACT.Abs, bias=ch[:, e, DT_B:DT_B + 1])
                last.then_inc(a_free[q % 2], 1)

            def soft_exps(c, par):
                act.wait_ge(a_free[0], A_JOBS * c + 6)
                act.wait_ge(a_free[1], A_JOBS * c + 6)
                act.activation(u[par][:, :, :], u[par][:, :, :], ACT.Exp, scale=-1.0).then_inc(soft_exp, 1)

            def soft_logs(c, par):
                act.wait_ge(soft_exp, c + 1)
                for h in range(2):
                    k = slice(h * KE // 2, (h + 1) * KE // 2)
                    act.activation(u[par][:, k, :], u[par][:, k, :], ACT.Ln, bias=1.0).then_inc(soft_ln, 1)

            def seam_decays(c, par):
                act.wait_ge(dt_made, 2 * c + 2)
                wait(act, ub_made, STEPS * (c - 1))
                for q in range(PAIRS):
                    e = 2 * q + 1
                    last = act.activation(seam[par][:, :, q], decay_rate[:, e, :], ACT.Exp, scale=dt[par][:, e, 0:1])
                last.then_inc(seam_decay, 1)

            def start_acc(c, par, j):
                t, eh = j // 2, j % 2
                act.wait_ge(a_full[j % 2], A_JOBS * c + 7 + j // 2)
                if isinstance(c, int) and c == 1:
                    act.wait_ge(stage_used[0], (len(STAGED) + 1) // 2)
                act.activation(acc[par][:, t, eh * HALF:(eh + 1) * HALF], bank_a[j % 2][:, :],
                               ACT.Copy).then_inc(a_free[j % 2], 1)

            def tanh_gate(c, q):
                act.wait_ge(c_full[q % 2], C_JOBS * c + q // 2 + 1)
                if q:
                    act.wait_ge(c_free[(q - 1) % 2], C_JOBS * c + (q - 1) // 2 + 1)
                act.activation(tanh_g[:, :], bank_c[q % 2][:, :], ACT.Tanh, scale=0.5).then_inc(tanh_g_made, 1)

            def z_after(c):
                normalize(c, nrm_c, xc, z2, norm_c, z_c)

            def modulate_after(c, par, j):
                act.wait_ge(c_full[j], C_JOBS * c + 6)
                if j == 0 and not (isinstance(c, int) and c >= CHUNKS - 2):
                    act.wait_ge(a_full[0], A_JOBS * (c + 2) + 1)
                    act.wait_ge(a_full[1], A_JOBS * (c + 2) + 1)
                modulate(bank_c[j], h2T, j, par, SB, CB).then_inc(c_free[j], 1)

            def rows_absolute(i):
                act.wait_ge(stage_used[i], 2)
                wait(act, rows_made, BATCH * i)
                for b in range(BATCH):
                    last = act.activation(xc[:, b, :], bank_c[b][:, :], ACT.Abs)
                last.then_inc(rows_abs, 1)

            act.wait_ge(small_loaded, 32)
            act.activation(decay_rate[:, :, :], ch[:, :, A_AT:], ACT.Exp).then_inc(rate_exp, 1)
            act.activation(cond_s[:, :, :], cond[:, :, :], ACT.Tanh, scale=0.5).then_inc(cond_tanh, 1)

            z_before(0)
            act.wait_ge(mods_made, 2)
            act.wait_ge(prep, 3)
            act.wait_ge(consts_made, 3)
            modulate_before(0, 0, 0)
            modulate_before(0, 0, 1)
            for q in range(PAIRS):
                copy_h(0, 0, q)
                tanh_before(0, q)
            for q in range(PAIRS):
                skip(0, q)
            copy_dt(0)
            copy_b_c(0, 0)
            for q in range(PAIRS):
                split_dt(0, 0, q)
            soft_exps(0, 0)
            soft_logs(0, 0)
            for j in range(2 * LB):
                start_acc(0, 0, j)
            act.wait_ge(prep, 5)
            seam_decays(0, 0)

            def one_round(c, par, la, lc):
                first = isinstance(c, int) and c == 0
                for s in range(STEPS):
                    decays(c, par, 2 * s)
                    decays(c, par, 2 * s + 1)
                    if s:
                        keep_carry(c, par, s - 1)
                    elif not first:
                        keep_carry(c - 1, 1 - par, STEPS - 1)
                    if first and s in (1, 3):
                        rows_absolute(s // 2)
                    if la is not None:
                        if s == 4:
                            z_before(c + 1)
                        if s == 6:
                            modulate_before(c + 1, 1 - par, 0)
                            modulate_before(c + 1, 1 - par, 1)
                        if s in (9, 11, 14, 16):
                            copy_h(c + 1, 1 - par, {9: 0, 11: 1, 14: 2, 16: 3}[s])
                        if s in (10, 12, 15, 17):
                            tanh_before(c + 1, {10: 0, 12: 1, 15: 2, 17: 3}[s])
                        if s in (17, 18):
                            skip(c + 1, s - 17)
                        if s == 18:
                            skip(c + 1, 2)
                        if s == 19:
                            copy_dt(c + 1)
                        if s == 23:
                            copy_b_c(c + 1, 1 - par)
                            skip(c + 1, 3)
                        if s in (20, 22, 24, 25):
                            split_dt(c + 1, 1 - par, {20: 0, 22: 2, 24: 1, 25: 3}[s])
                        if s == 26:
                            soft_exps(c + 1, 1 - par)
                        if s == 27:
                            soft_logs(c + 1, 1 - par)
                        if s in (29, 30):
                            start_acc(c + 1, 1 - par, 2 * (s - 29))
                            start_acc(c + 1, 1 - par, 2 * (s - 29) + 1)
                        if s == 31:
                            seam_decays(c + 1, 1 - par)
                    if lc is not None:
                        if s in (0, 1, 4, 6):
                            tanh_gate(c - 1, {0: 0, 1: 1, 4: 2, 6: 3}[s])
                        if s == 19:
                            z_after(c - 1)
                        if s == 21:
                            act.wait_ge(mods_made, 4)
                            modulate_after(c - 1, 1 - par, 0)
                            modulate_after(c - 1, 1 - par, 1)

            rounds(act, one_round)
            last = CHUNKS - 1
            for q in range(PAIRS):
                tanh_gate(last, q)
            z_after(last)
            modulate_after(last, 1, 0)
            modulate_after(last, 1, 1)

        @block.tensor
        def _(pe):
            def turn_states(c, g):
                s, q = g // 2, g % 2
                pe.wait_ge(scanned, UNITS * c + g + 1)
                if q == 0:
                    wait(pe, summed, STEPS * c + s)
                for j in range(2):
                    for t in range(LB):
                        at = (2 * q + j) * P
                        last = pe.transpose(turn[t][:, at:at + P], state[:, g % RING, j, t * P:(t + 1) * P], ident[:, :])
                last.then_inc(turned, 1)

            def turn_x(c, j):
                pe.wait_ge(z_a, c + 1)
                wait(pe, a_free[j], A_JOBS * c)
                for i in range(2):
                    for t in range(LB):
                        k = 2 * j + i
                        last = pe.transpose(bank_a[j][:, i * ROWS + t * P:i * ROWS + (t + 1) * P],
                                            xa[:, t, k * P:(k + 1) * P], ident[:, :])
                last.then_inc(a_full[j], 1)

            def project_in(dst, full, hTc, m0, q, j):
                m = m0 + 2 * q + j
                for k in range(KD):
                    last = pe.matmul(dst[:, j * ROWS:(j + 1) * ROWS], win[:, k, m * P:(m + 1) * P], hTc[:, k, :],
                                     start=(k == 0), stop=(k == KD - 1))
                if j == 1:
                    last.then_inc(full, 1)

            def project_h(c, par, q, j):
                if j == 0:
                    pe.wait_ge(a_free[q % 2], A_JOBS * c + 1 + q // 2)
                    if q == 0:
                        pe.wait_ge(a_free[1], A_JOBS * c + 1)
                project_in(bank_a[q % 2], a_full[q % 2], hT[par], 0, q, j)

            def project_dt(c, q):
                if q == 0:
                    pe.wait_ge(a_free[0], A_JOBS * c + 3)
                    pe.wait_ge(a_free[1], A_JOBS * c + 2)
                if q == PAIRS - 1:
                    pe.wait_ge(a_free[1], A_JOBS * c + 3)
                for k in (2 * q, 2 * q + 1):
                    last = pe.matmul(bank_a[0][:, 0:ROWS], xp[:, k, 0:RANK_DT], hc[:, k, :], start=(k == 0), stop=(k == KE - 1))
                if q == PAIRS - 1:
                    last.then_inc(a_full[0], 1)

            def project_b(c, h):
                for k in range(h * KE // 2, (h + 1) * KE // 2):
                    pe.matmul(bank_a[1][0:N, ROWS:2 * ROWS], xp[:, k, RANK_DT:RANK_DT + N], hc[:, k, :],
                              start=(k == 0), stop=(k == KE - 1))

            def project_c(c, t):
                for k in range(KE):
                    last = pe.matmul(bank_a[1][:, t * N:(t + 1) * N], hc[:, k, t * P:(t + 1) * P],
                                     xp[:, k, RANK_DT + N:], start=(k == 0), stop=(k == KE - 1))
                if t == LB - 1:
                    last.then_inc(a_full[1], 1)

            def expand_dt(c, q):
                pe.wait_ge(a_free[q % 2], A_JOBS * c + 4 + q // 2)
                for j in range(2):
                    m = 2 * q + j
                    last = pe.matmul(bank_a[q % 2][:, j * ROWS:(j + 1) * ROWS], dtw[:, m * P:(m + 1) * P], dtr[:, :],
                                     start=True, stop=True)
                last.then_inc(a_full[q % 2], 1)

            def turn_skip(c, j):
                t, eh = j // 2, j % 2
                pe.wait_ge(skip_made, PAIRS * (c + 1))
                pe.wait_ge(a_free[j % 2], A_JOBS * c + 6 + j // 2)
                for i in range(4):
                    last = pe.transpose(bank_a[j % 2][:, i * P:(i + 1) * P], yg[:, 4 * eh + i, t * P:(t + 1) * P],
                                        ident[:, :])
                last.then_inc(a_full[j % 2], 1)

            def project_gate(c, par, q, j):
                if j == 0:
                    wait(pe, c_free[q % 2], C_JOBS * c + q // 2)
                project_in(bank_c[q % 2], c_full[q % 2], hT[par], KE, q, j)

            def turn_sums(c, par, q):
                if q == 0:
                    pe.wait_ge(summed, STEPS * (c + 1))
                pe.wait_ge(c_free[q % 2], C_JOBS * c + 2 + q // 2)
                for j in range(2):
                    for t in range(LB):
                        m = 2 * q + j
                        last = pe.transpose(bank_c[q % 2][:, j * ROWS + t * P:j * ROWS + (t + 1) * P],
                                            acc[par][:, t, m * P:(m + 1) * P], ident[:, :])
                last.then_inc(c_full[q % 2], 1)

            def project_out(c, t, q):
                if q == 0:
                    pe.wait_ge(c_free[t], C_JOBS * c + 4)
                pe.wait_ge(c_free[q % 2], C_JOBS * c + 3 + q // 2)
                for k in (2 * q, 2 * q + 1):
                    last = pe.matmul(bank_c[t][:, :], yg[:, k, t * P:(t + 1) * P], wo[:, k, :],
                                     start=(k == 0), stop=(k == KE - 1))
                if q == PAIRS - 1:
                    last.then_inc(c_full[t], 1)

            def turn_z(c, j):
                pe.wait_ge(z_c, c + 1)
                pe.wait_ge(c_free[j], C_JOBS * c + 5)
                for i in range(2):
                    for t in range(LB):
                        k = 2 * j + i
                        last = pe.transpose(bank_c[j][:, i * ROWS + t * P:i * ROWS + (t + 1) * P],
                                            z2[:, t, k * P:(k + 1) * P], ident[:, :])
                last.then_inc(c_full[j], 1)

            def ffn_bias(c, t):
                pe.wait_ge(c_free[0], C_JOBS * c + 6)
                pe.wait_ge(c_free[1], C_JOBS * c + 6)
                pe.matmul(bank_c[t][:, :], ones_row[:, :], bias_row[:, :], start=True, stop=False)

            def project_ffn(c, t, ks):
                for k in ks:
                    last = pe.matmul(bank_c[t][:, :], h2T[:, k, t * P:(t + 1) * P], ffn[:, k, :],
                                     start=False, stop=(k == KD - 1))
                if k == KD - 1:
                    last.then_inc(c_full[t], 1)

            def mod_columns(j):
                pe.wait_ge(stage_loaded[j % 2], 16 * (j // 2 + 1))
                if j in (1, 5):
                    pe.wait_ge(mods_made, j // 4 * 2 + 1)
                if j == 4:
                    pe.wait_ge(rows_made, 2 * BATCH)
                for m in range(KD):
                    for k in range(KD):
                        last = pe.matmul(bank_c[0][:, m * BATCH:(m + 1) * BATCH], staged[j % 2][:, k, m * P:(m + 1) * P],
                                         cond_h[:, k, :], start=(k == 0), stop=(k == KD - 1))
                last.then_inc(stage_used[j % 2], 1)

            def mod_rows(j):
                pe.wait_ge(stage_loaded[j % 2], 16 * (j // 2 + 1))
                if j == 2:
                    pe.wait_ge(mods_made, 2)
                    pe.wait_ge(prep, 4)
                wait(pe, rows_made, BATCH * (j - 2))
                for b in range(BATCH):
                    for k in range(KD):
                        last = pe.matmul(bank_c[b][:, :], cond_all[:, k, b, :], staged[j % 2][:, k, :],
                                         start=(k == 0), stop=(k == KD - 1))
                last.then_inc(stage_used[j % 2], 1)

            pe.wait_ge(prep, 2)
            mod_columns(0)
            mod_columns(1)
            pe.wait_ge(consts_made, 3)
            turn_x(0, 0)
            turn_x(0, 1)
            pe.wait_ge(win_h_loaded, 16)
            for q in range(PAIRS):
                project_h(0, 0, q, 0)
                project_h(0, 0, q, 1)
            pe.wait_ge(xp_loaded, 32)
            for q in range(PAIRS):
                project_dt(0, q)
            for h in range(2):
                project_b(0, h)
            for t in range(LB):
                project_c(0, t)
            for q in range(PAIRS):
                expand_dt(0, q)
            for j in range(2 * LB):
                turn_skip(0, j)

            def one_round(c, par, la, lc):
                first = isinstance(c, int) and c == 0
                for s in range(STEPS):
                    turn_states(c, 2 * s)
                    turn_states(c, 2 * s + 1)
                    if first:
                        if s in (0, 2):
                            mod_rows(2 + s // 2)
                        if s in (4, 5):
                            mod_columns(s)
                        if s == 27:
                            pe.wait_ge(mods_made, 4)
                            pe.wait_ge(rows_made, 2 * BATCH)
                            pe.wait_ge(late_loaded, 64)
                            pe.wait_ge(bias_scaled, 1)
                            pe.wait_ge(stage_used[0], (len(STAGED) + 1) // 2)
                    if la is not None:
                        if s == 4:
                            turn_x(c + 1, 0)
                            turn_x(c + 1, 1)
                        if 6 <= s <= 9:
                            project_h(c + 1, 1 - par, (s - 6) // 2, s % 2)
                        if 11 <= s <= 14:
                            project_h(c + 1, 1 - par, (s - 7) // 2, (s - 7) % 2)
                        if s == 16:
                            project_dt(c + 1, 0)
                            project_dt(c + 1, 1)
                        if s in (17, 18):
                            project_dt(c + 1, s - 15)
                        if s in (18, 19):
                            project_b(c + 1, s - 18)
                        if s in (19, 20, 23, 24):
                            expand_dt(c + 1, {19: 0, 20: 2, 23: 1, 24: 3}[s])
                        if s in (20, 21):
                            project_c(c + 1, s - 20)
                        if s in (26, 29):
                            turn_skip(c + 1, 2 * (s // 29))
                            turn_skip(c + 1, 2 * (s // 29) + 1)
                    if lc is not None:
                        if 1 <= s <= 4:
                            project_gate(c - 1, 1 - par, (s + 3) // 2, (s + 3) % 2)
                        if s == 5:
                            turn_sums(c - 1, 1 - par, 0)
                        if s == 7:
                            turn_sums(c - 1, 1 - par, 1)
                            turn_sums(c - 1, 1 - par, 2)
                        if s == 9:
                            turn_sums(c - 1, 1 - par, 3)
                            project_out(c - 1, 0, 0)
                        if s == 10:
                            project_out(c - 1, 0, 1)
                            project_out(c - 1, 0, 2)
                        if s == 11:
                            project_out(c - 1, 0, 3)
                        if 12 <= s <= 15:
                            project_out(c - 1, 1, s - 12)
                        if s == 19:
                            turn_z(c - 1, 0)
                            turn_z(c - 1, 1)
                        if s in (21, 24):
                            ffn_bias(c - 1, s // 24)
                            project_ffn(c - 1, s // 24, (0,))
                        if s in (22, 25):
                            project_ffn(c - 1, s // 25, (1, 2))
                        if s in (23, 26):
                            project_ffn(c - 1, s // 26, (3,))
                    if 27 <= s <= 30:
                        project_gate(c, par, (s - 27) // 2, (s - 27) % 2)

            rounds(pe, one_round)
            last = CHUNKS - 1
            for q in (2, 3):
                project_gate(last, 1, q, 0)
                project_gate(last, 1, q, 1)
            for q in range(PAIRS):
                turn_sums(last, 1, q)
            for t in range(LB):
                for q in range(PAIRS):
                    project_out(last, t, q)
            turn_z(last, 0)
            turn_z(last, 1)
            for t in range(LB):
                ffn_bias(last, t)
                project_ffn(last, t, range(KD))

        @block.vector
        def _(dve):
            def scan(c, par, g):
                n, q = g // PAIRS, g % PAIRS
                dve.wait_ge(decay_made, UNITS * c + g + 1)
                if g % 2 == 0:
                    dve.wait_ge(ub_made, STEPS * c + g // 2 + 1)
                wait(dve, turned, UNITS * c + g - RING + 1)
                wait(dve, carried, STEPS * c + (g - RING) // 2 + 1)
                dve.tensor_tensor_scan(state[:, g % RING, :, :].rearrange("p j r -> p (j r)"), decay[g % 2][:, :],
                                       ub[:, g % RING, :, :].rearrange("p j r -> p (j r)"),
                                       carry[par][:, n, 2 * q:2 * q + 1], ALU.mult, ALU.add).then_inc(scanned, 1)

            def add_states(c, par, s):
                n, eh = s // 2, s % 2
                if s == 0:
                    dve.wait_ge(a_free[0], A_JOBS * (c + 1))
                    dve.wait_ge(a_free[1], A_JOBS * (c + 1))
                dve.wait_ge(turned, UNITS * c + 2 * s + 2)
                wait(dve, summed, STEPS * c + s - 1)
                for t in range(LB):
                    part = acc[par][:, t, eh * HALF:(eh + 1) * HALF]
                    last = dve.scalar_tensor_tensor(out=part, in0=turn[t][:, :], scalar=c_rows[par][:, t, n:n + 1],
                                                    in1=part, op0=ALU.mult, op1=ALU.add)
                last.then_inc(summed, 1)

            def stats(c, src, stat, bn, used):
                wait(dve, used, 4 * c)
                for t in range(LB):
                    last = dve.bn_stats(stat[:, t, :], src[:, t, :])
                last.then_inc(bn, 1)

            def means(stat, mv, done):
                for t in range(LB):
                    last = dve.bn_aggr(mv[:, t, :], stat[:, t, :])
                last.then_inc(done, 1)

            def stats_before(c):
                dve.wait_ge(xa_loaded, 16 * c + 16)
                stats(c, xa, stat_a, bn_a, norm_a)

            def taps(c, q):
                bk = bank_a[q % 2]
                dve.wait_ge(pre_made, PAIRS * c + q + 1)
                for k in range(TAPS - 1):
                    for j in range(2):
                        e, part = 2 * q + j, bk[:, j * ROWS:(j + 1) * ROWS]
                        if k:
                            dve.wait_ge(tap_done, 6 * (4 * c + q) + 2 * (k - 1) + j + 1)
                        dve.scalar_tensor_tensor(out=part, in0=pre[q % 2][:, j, k:k + ROWS], scalar=conv[:, e, k:k + 1],
                                                 in1=part, op0=ALU.mult, op1=ALU.add).then_inc(tap_done, 1)

            def silu_before(c, q):
                dve.wait_ge(tanh_h_made, PAIRS * c + q + 1)
                if q == 0:
                    wait(dve, u_made, 2 * c)
                    wait(dve, skip_made, PAIRS * c)
                dve.scalar_tensor_tensor(out=hc[:, 2 * q:2 * q + 2, :].rearrange("p k r -> p (k r)"), in0=tanh_h[:, :],
                                         scalar=1.0, in1=bank_a[q % 2][:, :], op0=ALU.add,
                                         op1=ALU.mult).then_inc(a_free[q % 2], 1)

            def add_dt(c, par, h):
                k = slice(h * KE // 2, (h + 1) * KE // 2)
                dve.wait_ge(soft_ln, 2 * c + h + 1)
                dve.tensor_tensor(dt[par][:, k, :], dt[par][:, k, :], u[par][:, k, :], ALU.add).then_inc(dt_made, 1)

            def silu_gate(c, q):
                if q == 0:
                    done = min(c + 2, CHUNKS) if isinstance(c, int) else c + 2
                    dve.wait_ge(a_full[0], A_JOBS * done)
                    dve.wait_ge(a_full[1], A_JOBS * done)
                dve.wait_ge(tanh_g_made, PAIRS * c + q + 1)
                dve.scalar_tensor_tensor(out=yg[:, 2 * q:2 * q + 2, :].rearrange("p k r -> p (k r)"), in0=tanh_g[:, :],
                                         scalar=1.0, in1=bank_c[q % 2][:, :], op0=ALU.add,
                                         op1=ALU.mult).then_inc(c_free[q % 2], 1)

            def gate_sums(c, q):
                dve.wait_ge(c_full[q % 2], C_JOBS * c + 3 + q // 2)
                part = yg[:, 2 * q:2 * q + 2, :].rearrange("p k r -> p (k r)")
                dve.tensor_tensor(part, bank_c[q % 2][:, :], part, ALU.mult).then_inc(c_free[q % 2], 1)

            def residual(c, t, job, gates, par, chain):
                dve.wait_ge(c_full[t], C_JOBS * c + job)
                dve.tensor_tensor(bank_c[t][:, :], bank_c[t][:, :], gates[:, par, :], ALU.mult).then_inc(chain, 1)
                dve.wait_ge(chain, LB * c + t + 1)
                dve.tensor_tensor(xc[:, t, :], bank_c[t][:, :], xc[:, t, :], ALU.add).then_inc(c_free[t], 1)

            def residual_mixer(c, par, t):
                if t == 0:
                    dve.wait_ge(xc_loaded, 16 * c + 16)
                residual(c, t, 5, ga, par, o_scaled)

            def stats_after(c):
                dve.wait_ge(c_free[0], C_JOBS * c + 5)
                dve.wait_ge(c_free[1], C_JOBS * c + 5)
                stats(c, xc, stat_c, bn_c, norm_c)

            def residual_ffn(c, par, t):
                residual(c, t, 7, gb, par, f_scaled)

            def copy_mods(j, kind):
                dve.wait_ge(stage_used[j % 2], j // 2 + 1)
                dst = mods[:, kind, :, :].rearrange("p k b -> p (k b)")
                one = 1.0 if kind in (CA, CB) else 0.0
                dve.tensor_scalar(dst, bank_c[0][:, 0:KD * BATCH], one, None, ALU.add).then_inc(mods_made, 1)

            def clamp_rows(i, gates, factor):
                dve.wait_ge(rows_abs, i + 1)
                for b in range(BATCH):
                    n = 2 * BATCH * i + 2 * b
                    g = gates[:, b, :]
                    dve.tensor_scalar(g, bank_c[b][:, :], 0.0, 2.0 * factor, ALU.is_ge, ALU.mult).then_inc(rows_sign, 1)
                    dve.wait_ge(rows_sign, n + 1)
                    dve.tensor_scalar(g, g, -factor, None, ALU.add).then_inc(rows_sign, 1)
                    dve.wait_ge(rows_sign, n + 2)
                    dve.scalar_tensor_tensor(out=g, in0=xc[:, b, :], scalar=0.25, in1=g, op0=ALU.max,
                                             op1=ALU.mult).then_inc(rows_made, 1)

            def add_factor(j):
                dve.wait_ge(stage_loaded[j % 2], 16 * (j // 2 + 1))
                if j > MODS:
                    dve.wait_ge(stage_used[(j - 1) % 2], (j - 1) // 2 + 1)
                dve.tensor_tensor(ffn[:, :, :], ffn[:, :, :], staged[j % 2], ALU.add).then_inc(stage_used[j % 2], 1)

            dve.wait_ge(cond_tanh, 1)
            dve.scalar_tensor_tensor(out=cond_s[:, :, :], in0=cond_s[:, :, :], scalar=1.0, in1=cond[:, :, :],
                                     op0=ALU.add, op1=ALU.mult).then_inc(prep, 1)
            dve.wait_ge(prep, 1)
            dve.tensor_scalar(cond_h[:, :, :], cond_s[:, :, :], 0.5, None, ALU.mult).then_inc(prep, 1)
            dve.tensor_scalar(conv[:, :, :], ch[:, :, 0:TAPS + 1], 0.5, None, ALU.mult).then_inc(prep, 1)
            stats_before(0)
            dve.wait_ge(bn_a, 1)
            means(stat_a, mv_a, stats_a)
            copy_mods(0, SA)
            copy_mods(1, CA)
            dve.wait_ge(prep, 2)
            dve.tensor_copy(cond_all, cond_h[:, :, :].unsqueeze(3).to_broadcast([P, KD, BATCH, P])).then_inc(prep, 1)
            dve.wait_ge(rate_exp, 1)
            dve.tensor_scalar(decay_rate[:, :, :], decay_rate[:, :, :], -1.0, None, ALU.mult).then_inc(prep, 1)
            for i in range(2):
                last = dve.memset(decay[i][:, ROWS:ROWS + 1], 0.0)
            last.then_inc(seam_zeroed, 1)
            for q in range(PAIRS):
                taps(0, q)
                silu_before(0, q)
            add_dt(0, 0, 0)
            add_dt(0, 0, 1)
            dve.wait_ge(seam_zeroed, 1)

            def one_round(c, par, la, lc):
                first = isinstance(c, int) and c == 0
                for s in range(STEPS):
                    if la is not None and s == 3:
                        dve.wait_ge(bn_a, c + 2)
                    if lc is not None and s == 18:
                        dve.wait_ge(bn_c, c)
                    scan(c, par, 2 * s)
                    if la is not None and s == 3:
                        means(stat_a, mv_a, stats_a)
                    if lc is not None and s == 18:
                        means(stat_c, mv_c, stats_c)
                    if s:
                        add_states(c, par, s - 1)
                    elif not first:
                        add_states(c - 1, 1 - par, STEPS - 1)
                    scan(c, par, 2 * s + 1)
                    if first:
                        if s in (1, 3):
                            clamp_rows(s // 2, *[(ga, 0.5), (gb, RANK ** -0.5)][s // 2])
                        if s in (5, 6):
                            copy_mods(s - 1, (SB, CB)[s - 5])
                        if MODS < s < MODS + RANK:
                            add_factor(s - 1)
                        if s == MODS + RANK:
                            dve.wait_ge(late_loaded, 64)
                            dve.tensor_scalar(bias_row[:, :], bias_row[:, :], math.sqrt(RANK), None,
                                              ALU.mult).then_inc(bias_scaled, 1)
                    if lc is not None:
                        if s in (0, 1, 4, 6):
                            silu_gate(c - 1, {0: 0, 1: 1, 4: 2, 6: 3}[s])
                        if s == 6:
                            gate_sums(c - 1, 0)
                        if s == 8:
                            gate_sums(c - 1, 1)
                            gate_sums(c - 1, 2)
                        if s == 10:
                            gate_sums(c - 1, 3)
                        if s in (13, 17):
                            residual_mixer(c - 1, 1 - par, s // 17)
                        if s == 17:
                            stats_after(c - 1)
                        if s in (26, 27):
                            residual_ffn(c - 1, 1 - par, s - 26)
                    if la is not None:
                        if s == 2:
                            stats_before(c + 1)
                        if s in (9, 11, 14, 16):
                            taps(c + 1, {9: 0, 11: 1, 14: 2, 16: 3}[s])
                        if s in (10, 12, 15, 17):
                            silu_before(c + 1, {10: 0, 12: 1, 15: 2, 17: 3}[s])
                        if s == 28:
                            add_dt(c + 1, 1 - par, 0)
                            add_dt(c + 1, 1 - par, 1)

            rounds(dve, one_round)
            last = CHUNKS - 1
            add_states(last, 1, STEPS - 1)
            for q in range(PAIRS):
                silu_gate(last, q)
            for q in range(PAIRS):
                gate_sums(last, q)
            residual_mixer(last, 1, 0)
            residual_mixer(last, 1, 1)
            stats_after(last)
            dve.wait_ge(bn_c, CHUNKS)
            means(stat_c, mv_c, stats_c)
            residual_ffn(last, 1, 0)
            residual_ffn(last, 1, 1)


def kernel(**inputs):
    import numpy as np
    import concourse.bacc as bacc
    from concourse.bass_utils import run_bass_kernel_spmd

    def tiles(a):
        a = np.asarray(a)
        return a.reshape(a.shape[0] // P, P, -1).transpose(1, 0, 2)

    at = {k.removeprefix("L0_"): np.asarray(v) for k, v in inputs.items()}
    chan = np.concatenate([tiles(at[k]) for k in ("attn_conv_w", "attn_conv_b", "attn_dt_proj_b", "attn_D", "attn_A_log")], axis=2)
    arrays = {
        "x": at["attn_hidden_states"], "win_t": at["attn_in_proj_w"].T, "xp_t": at["attn_x_proj_w"].T,
        "dt_t": at["attn_dt_proj_w"].T, "wo_t": at["attn_out_proj_w"].T, "chan": chan,
        "cond_t": tiles(at["c"].T), "wmod": at["wmod"], "factors": at["ffn_factors"], "bias": at["ffn_bias"],
    }
    arrays = {k: np.ascontiguousarray(v) for k, v in arrays.items()}
    nc = bacc.Bacc("TRN2", target_bir_lowering=False, num_devices=1)
    args = [nc.dram_tensor(k, v.shape, mybir.dt.from_np(v.dtype), kind="ExternalInput").ap() for k, v in arrays.items()]
    out = nc.dram_tensor("out", (BATCH, SEQ, DIM), F32, kind="ExternalOutput").ap()
    build(nc, *args, out)
    r = run_bass_kernel_spmd(nc, [arrays], core_ids=[0])
    return r.results[0]["out"]
```

```python
from contextlib import ExitStack
import math

import concourse.bass as bass
from concourse import mybir

F32 = mybir.dt.float32
ALU = mybir.AluOpType
ACT = mybir.ActivationFunctionType

P = 128
BATCH, SEQ, DIM = 2, 2048, 512
E, N, TAPS, RANK_DT = 1024, 16, 4, 128
RANK = 8
EPS = 1e-5
ROWS = 256
LB = ROWS // P
CHUNKS = BATCH * SEQ // ROWS
KD = DIM // P
KE = E // P
PAIRS = KE // 2
UNITS = N * PAIRS
STEPS = UNITS // 2
HALF = E // 2
RING = 4
UB_RING = 8
CONV_B, DT_B, SKIP, A_AT = TAPS, TAPS + 1, TAPS + 2, TAPS + 3
CHAN = A_AT + N
SA, CA, SB, CB = range(4)
STAGED = [0, 1, 2, 5, 3, 4] + list(range(1, RANK))
MODS = 6
A_JOBS, C_JOBS = (8, 9), 7


def wait(eng, sem, value):
    if not (isinstance(value, int) and value <= 0):
        eng.wait_ge(sem, value)


def build(nc, x, win_t, xp_t, dt_t, wo_t, chan, cond_t, wmod, factors, bias, out):
    x_rows = x.rearrange("b (n t p) d -> b n p t d", t=LB, p=P)
    out_rows = out.rearrange("b (n t p) d -> b n p t d", t=LB, p=P)
    win_v = win_t.rearrange("(k p) e -> p k e", p=P)
    xp_v = xp_t.rearrange("(k p) r -> p k r", p=P)
    wo_v = wo_t.rearrange("(k p) d -> p k d", p=P)
    wmod_v = wmod.rearrange("(k p) (j d) -> j p k d", p=P, j=MODS)
    fac_v = factors.rearrange("r (k p) d -> r p k d", p=P)
    b_dram = nc.dram_tensor("b_scratch", (2, N * ROWS), F32).ap()

    with ExitStack() as ctx:
        def sb(name, shape):
            return ctx.enter_context(nc.sbuf_tensor(name, shape, F32))

        def bank(name):
            return ctx.enter_context(nc.psum_tensor(name, [P, 512], F32))

        def sem(name):
            return ctx.enter_context(nc.semaphore(name))

        win = sb("win", [P, KD, 2 * E])
        xp = sb("xp", [P, KE, RANK_DT + 2 * N])
        dtw = sb("dtw", [P, E])
        wo = sb("wo", [P, KE, DIM])
        ffn = sb("ffn", [P, KD, DIM])
        ga = sb("ga", [P, BATCH, DIM])
        gb = sb("gb", [P, BATCH, DIM])
        ident = sb("ident", [P, P])
        ch = sb("ch", [P, KE, CHAN])
        conv = sb("conv", [P, KE, TAPS + 1])
        decay_rate = sb("decay_rate", [P, KE, N])
        mods = sb("mods", [P, 4, KD, BATCH])
        cond = sb("cond", [P, KD, BATCH])
        cond_s = sb("cond_s", [P, KD, BATCH])
        cond_h = sb("cond_h", [P, KD, BATCH])
        small = sb("small", [P, 3, LB])
        ones_row = sb("ones_row", [1, P])
        bias_row = sb("bias_row", [1, DIM])
        xa = sb("xa", [P, LB, DIM])
        hT = [sb(f"hT{i}", [P, KD, ROWS]) for i in range(2)]
        pre_z = sb("pre_z", [P, 2 * 2 * (TAPS - 1 + ROWS)])
        pre = [pre_z[:, i * 2 * (TAPS - 1 + ROWS):(i + 1) * 2 * (TAPS - 1 + ROWS)].rearrange("p (j r) -> p j r", j=2)
               for i in range(2)]
        hist = [sb(f"hist{i}", [P, KE, TAPS - 1]) for i in range(BATCH)]
        tanh_s = sb("tanh_s", [P, 512])
        hc = sb("hc", [P, KE, ROWS])
        dtr = tanh_s[:, 0:ROWS]
        bc_s = tanh_s[0:2 * N, ROWS:2 * ROWS]
        stat_a = sb("stat_a", [P, LB, 6])
        mv_a = sb("mv_a", [P, LB, 2])
        nrm_a = sb("nrm_a", [P, 4, LB])
        dt = [sb(f"dt{i}", [P, KE, ROWS]) for i in range(2)]
        u = [sb(f"u{i}", [P, KE, ROWS]) for i in range(2)]
        b_all = sb("b_all", [P, N, ROWS])
        c_rows = [sb(f"c_rows{i}", [P, LB, N]) for i in range(2)]
        ub = sb("ub", [P, UB_RING, 2, ROWS])
        state = sb("state", [P, RING, 2, ROWS])
        carry = [sb(f"carry{i}", [P, N, KE]) for i in range(BATCH)]
        seam = [sb(f"seam{i}", [P, N, PAIRS]) for i in range(2)]
        acc = [sb(f"acc{i}", [P, LB, E]) for i in range(2)]
        xc = sb("xc", [P, LB, DIM])
        yg = sb("yg", [P, KE, ROWS])
        z2 = pre_z[:, 0:LB * DIM].rearrange("p (t d) -> p t d", t=LB)
        h2T = xa[:, :, :].rearrange("p t d -> p (t d)").rearrange("p (k r) -> p k r", k=KD)
        stat_c = sb("stat_c", [P, LB, 6])
        mv_c = sb("mv_c", [P, LB, 2])
        nrm_c = sb("nrm_c", [P, 4, LB])
        staged = [acc[1][:, :, :].rearrange("p t e -> p (t e)").rearrange("p (k d) -> p k d", k=KD),
                  yg[:, :, :].rearrange("p k r -> p (k r)").rearrange("p (k d) -> p k d", k=KD)]
        cond_all = b_all[:, N // 2:N // 2 + KD, :].rearrange("p k (b q) -> p k b q", b=BATCH)

        decay = [bank(f"decay{i}") for i in range(2)]
        turn = [bank(f"turn{i}") for i in range(LB)]
        bank_a = [bank(f"bank_a{i}") for i in range(2)]
        bank_c = [bank(f"bank_c{i}") for i in range(2)]

        ub_made, decay_made, scanned, turned = sem("ub_made"), sem("decay_made"), sem("scanned"), sem("turned")
        summed, carried = sem("summed"), sem("carried")
        ub_product, seam_decay, seam_made, seam_zeroed = sem("ub_product"), sem("seam_decay"), sem("seam_made"), sem("seam_zeroed")
        a_full = [sem(f"a_full{i}") for i in range(2)]
        a_free = [sem(f"a_free{i}") for i in range(2)]
        c_full = [sem(f"c_full{i}") for i in range(2)]
        c_free = [sem(f"c_free{i}") for i in range(2)]
        xa_loaded, bn_a, stats_a, norm_a, z_a = sem("xa_loaded"), sem("bn_a"), sem("stats_a"), sem("norm_a"), sem("z_a")
        pre_made, tap_done, tanh_h_made, skip_made = sem("pre_made"), sem("tap_done"), sem("tanh_h_made"), sem("skip_made")
        pair_read = sem("pair_read")
        soft_exp, soft_ln, dt_made, u_made = sem("soft_exp"), sem("soft_ln"), sem("dt_made"), sem("u_made")
        b_stored, h_copied = sem("b_stored"), sem("h_copied")
        b_loaded = [sem(f"b_loaded{i}") for i in range(2)]
        xc_loaded, bn_c, stats_c, norm_c, z_c = sem("xc_loaded"), sem("bn_c"), sem("stats_c"), sem("norm_c"), sem("z_c")
        tanh_g_made, o_scaled, result_made, out_stored = sem("tanh_g_made"), sem("o_scaled"), sem("result_made"), sem("out_stored")
        small_loaded, win_h_loaded, xp_loaded, late_loaded = sem("small_loaded"), sem("win_h_loaded"), sem("xp_loaded"), sem("late_loaded")
        stage_loaded = [sem(f"stage_loaded{i}") for i in range(2)]
        stage_used = [sem(f"stage_used{i}") for i in range(2)]
        consts_made, rate_exp, cond_tanh, prep = sem("consts_made"), sem("rate_exp"), sem("cond_tanh"), sem("prep")
        bias_scaled = sem("bias_scaled")
        mods_made, rows_abs, rows_sign, rows_made, ident_set = sem("mods_made"), sem("rows_abs"), sem("rows_sign"), sem("rows_made"), sem("ident_set")

        block = ctx.enter_context(nc.Block())

        def rounds(eng, one_round):
            one_round(0, 0, 0, None)
            with eng.Fori(0, CHUNKS // 2 - 1) as i:
                one_round(2 * i + 1, 1, i + 1, i)
                one_round(2 * i + 2, 0, i + 1, i)
            one_round(CHUNKS - 1, 1, None, CHUNKS // 2 - 1)

        @block.sync
        def _(sp):
            def load_stage(j):
                src = wmod_v[STAGED[j]] if j < MODS else fac_v[STAGED[j]]
                if j >= 2:
                    sp.wait_ge(stage_used[j % 2], j // 2)
                if j == 3:
                    sp.wait_ge(a_full[0], A_JOBS[0])
                    sp.wait_ge(a_full[1], A_JOBS[1])
                sp.dma_start(staged[j % 2], src).then_inc(stage_loaded[j % 2], 16)

            def store_b(c, par):
                sp.wait_ge(a_free[1], A_JOBS[1] * c + 4)
                sp.dma_start(b_dram[par].rearrange("(n r) -> n r", n=N), bc_s[0:N, :]).then_inc(b_stored, 16)

            def load_b(c, par, h):
                wait(sp, ub_made, STEPS * (c - 1) + (h + 1) * STEPS // 2)
                sp.wait_ge(b_stored, 16 * c + 16)
                if isinstance(c, int) and c == 0 and h == 1:
                    sp.wait_ge(stage_used[0], 2)
                    sp.wait_ge(stage_used[1], 2)
                n0 = h * N // 2
                src = b_dram[par:par + 1, n0 * ROWS:(n0 + N // 2) * ROWS].to_broadcast([P, N * ROWS // 2])
                sp.dma_start(b_all[:, n0:n0 + N // 2, :].rearrange("p n r -> p (n r)"), src).then_inc(b_loaded[h], 16)

            sp.dma_start(ch[:, :, :], chan).then_inc(small_loaded, 16)
            sp.dma_start(cond[:, :, :], cond_t).then_inc(small_loaded, 16)
            sp.dma_start(xa[:, :, :], x_rows[0, 0]).then_inc(xa_loaded, 16)
            load_stage(0)
            load_stage(1)
            sp.dma_start(win[:, :, 0:E], win_v[:, :, 0:E]).then_inc(win_h_loaded, 16)
            sp.dma_start(xp[:, :, :], xp_v).then_inc(xp_loaded, 16)
            sp.dma_start(dtw[:, :], dt_t).then_inc(xp_loaded, 16)
            sp.dma_start(win[:, :, E:2 * E], win_v[:, :, E:2 * E]).then_inc(late_loaded, 16)
            sp.dma_start(wo[:, :, :], wo_v).then_inc(late_loaded, 16)
            sp.dma_start(ffn[:, :, :], fac_v[0]).then_inc(late_loaded, 16)
            sp.dma_start(bias_row[:, :], bias.rearrange("(a d) -> a d", a=1)).then_inc(late_loaded, 16)
            store_b(0, 0)
            load_b(0, 0, 0)

            def one_round(c, par, la, lc):
                if la is not None:
                    sp.wait_ge(xa_loaded, 16)
                    if isinstance(c, int) and c == 0:
                        sp.wait_ge(a_full[1], 1)
                        sp.wait_ge(a_full[0], 1)
                    else:
                        sp.wait_ge(c_full[0], C_JOBS * (c - 1) + 1)
                    sp.dma_start(xa[:, :, :], x_rows[1 - par, la]).then_inc(xa_loaded, 16)
                if lc is not None:
                    sp.wait_ge(rows_made, 2 * BATCH)
                    wait(sp, out_stored, 16 * (c - 1))
                    sp.dma_start(xc[:, :, :], x_rows[1 - par, lc]).then_inc(xc_loaded, 16)
                if isinstance(c, int) and c == 0:
                    for j in range(2, 5):
                        load_stage(j)
                load_b(c, par, 1)
                if isinstance(c, int) and c == 0:
                    for j in range(5, len(STAGED)):
                        load_stage(j)
                if la is not None:
                    store_b(c + 1, 1 - par)
                    load_b(c + 1, 1 - par, 0)
                if lc is not None:
                    store_out(c - 1, 1 - par, lc)

            def store_out(c, par, lc):
                sp.wait_ge(result_made, c + 1)
                sp.dma_start(out_rows[par, lc], xc[:, :, :]).then_inc(out_stored, 16)

            rounds(sp, one_round)
            last = CHUNKS - 1
            sp.wait_ge(out_stored, 16 * last)
            sp.dma_start(xc[:, :, :], x_rows[1, CHUNKS // 2 - 1]).then_inc(xc_loaded, 16)
            store_out(last, 1, CHUNKS // 2 - 1)
            sp.wait_ge(out_stored, 16 * CHUNKS)
            sp.wait_ge(b_stored, 16 * CHUNKS)

        @block.gpsimd
        def _(pool):
            pool.memset(ident[:, :], 1.0).then_inc(ident_set, 1)
            pool.wait_ge(ident_set, 1)
            pool.affine_select(out=ident[:, :], in_=ident[:, :], compare_op=ALU.is_equal, fill=0.0, base=0,
                               pattern=[[-1, P]], channel_multiplier=1).then_inc(consts_made, 1)
            for i, value in enumerate((-0.5, EPS, -1.0)):
                last = pool.memset(small[:, i, :], value)
            last.then_inc(ident_set, 1)
            for b in range(BATCH):
                pool.memset(carry[b][:, :, :], 0.0)
                last = pool.memset(hist[b][:, :, :], 0.0)
            last.then_inc(consts_made, 1)
            pool.memset(ones_row[:, :], 1.0).then_inc(consts_made, 1)
            pool.wait_ge(ident_set, 2)

            def norm(c, mv, nrm, stats, chain, used):
                pool.wait_ge(stats, c + 1)
                wait(pool, used, c)
                pool.tensor_tensor(nrm[:, 0, :], mv[:, :, 1], small[:, 1, :], ALU.add).then_inc(chain, 1)
                pool.tensor_tensor(nrm[:, 1, :], mv[:, :, 0], small[:, 2, :], ALU.mult).then_inc(chain, 1)
                pool.wait_ge(chain, 4 * c + 2)
                pool.tensor_tensor(nrm[:, 2, :], nrm[:, 0, :], small[:, 0, :], ALU.pow).then_inc(chain, 1)
                pool.wait_ge(chain, 4 * c + 3)
                pool.tensor_tensor(nrm[:, 3, :], nrm[:, 1, :], nrm[:, 2, :], ALU.mult).then_inc(chain, 1)

            def norm_before(c):
                norm(c, mv_a, nrm_a, stats_a, norm_a, z_a)

            def norm_after(c):
                norm(c, mv_c, nrm_c, stats_c, norm_c, z_c)

            def add_ffn(c):
                pool.wait_ge(c_free[0], C_JOBS * (c + 1))
                pool.wait_ge(c_free[1], C_JOBS * (c + 1))
                pool.tensor_tensor(xc[:, :, :], xc[:, :, :], z2[:, :, :], ALU.add).then_inc(result_made, 1)

            def make_u(c, par, h):
                k = slice(h * KE // 2, (h + 1) * KE // 2)
                pool.wait_ge(dt_made, 2 * c + h + 1)
                pool.tensor_tensor(u[par][:, k, :], dt[par][:, k, :], hc[:, k, :], ALU.mult).then_inc(u_made, 1)

            def make_seam(c, par):
                pool.wait_ge(seam_decay, c + 1)
                wait(pool, carried, STEPS * (c - 1))
                odd = carry[par][:, :, :].rearrange("p n (q j) -> p n q j", j=2)[:, :, :, 1]
                pool.tensor_tensor(seam[par][:, :, :], seam[par][:, :, :], odd, ALU.mult).then_inc(seam_made, 1)

            def make_ub(c, par, s):
                n, q, slot = s // 2, 2 * (s % 2), 2 * s % UB_RING
                if s == 0:
                    pool.wait_ge(u_made, 2 * c + 2)
                if s % (STEPS // 2) == 0:
                    pool.wait_ge(b_loaded[s // (STEPS // 2)], 16 * c + 16)
                wait(pool, scanned, UNITS * c + 2 * s - UB_RING + 2)
                product = ub[:, slot:slot + 2, :, :].rearrange("p g j r -> p (g j) r")
                pool.tensor_tensor(product, u[par][:, 2 * q:2 * q + 4, :],
                                   b_all[:, n:n + 1, :].to_broadcast([P, 4, ROWS]), ALU.mult).then_inc(ub_product, 1)
                if s == 0:
                    make_seam(c, par)
                    pool.wait_ge(seam_made, c + 1)
                pool.wait_ge(ub_product, STEPS * c + s + 1)
                first = ub[:, slot:slot + 2, 1, 0]
                pool.tensor_tensor(first, first, seam[par][:, n, q:q + 2], ALU.add).then_inc(ub_made, 1)

            norm_before(0)
            make_u(0, 0, 0)
            make_u(0, 0, 1)

            def one_round(c, par, la, lc):
                for s in range(STEPS):
                    make_ub(c, par, s)
                    if la is not None:
                        if s == 4:
                            norm_before(c + 1)
                        if s == 31:
                            make_u(c + 1, 1 - par, 0)
                            make_u(c + 1, 1 - par, 1)
                    if lc is not None and s == 21:
                        norm_after(c - 1)
                    if lc is not None and s == 29:
                        add_ffn(c - 1)

            rounds(pool, one_round)
            norm_after(CHUNKS - 1)
            add_ffn(CHUNKS - 1)

        @block.scalar
        def _(act):
            def decays(c, par, g):
                n, q = g // PAIRS, g % PAIRS
                if g == 0:
                    act.wait_ge(dt_made, 2 * c + 2)
                wait(act, scanned, UNITS * c + g - 1)
                for j in range(2):
                    e = 2 * q + j
                    last = act.activation(decay[g % 2][:, j * ROWS + j:(j + 1) * ROWS], dt[par][:, e, j:], ACT.Exp,
                                          scale=decay_rate[:, e, n:n + 1])
                last.then_inc(decay_made, 1)

            def keep_carry(c, par, s):
                n, eh, slot = s // 2, s % 2, 2 * (s % 2)
                act.wait_ge(scanned, UNITS * c + 2 * s + 2)
                act.activation(carry[par][:, n, 4 * eh:4 * eh + 4].rearrange("p (a j) -> p a j", a=2),
                               state[:, slot:slot + 2, :, ROWS - 1], ACT.Copy).then_inc(carried, 1)

            def normalize(c, nrm, src, dst, chain, done):
                act.wait_ge(chain, 4 * c + 4)
                for t in range(LB):
                    last = act.activation(dst[:, t, :], src[:, t, :], ACT.Identity,
                                          bias=nrm[:, 3, t:t + 1], scale=nrm[:, 2, t:t + 1])
                last.then_inc(done, 1)

            def modulate(src, dst, j, b, shift, scale):
                for i in range(2):
                    k = 2 * j + i
                    last = act.activation(dst[:, k, :], src[:, i * ROWS:(i + 1) * ROWS], ACT.Identity,
                                          bias=mods[:, shift, k, b:b + 1], scale=mods[:, scale, k, b:b + 1])
                return last

            def z_before(c):
                normalize(c, nrm_a, xa, xa, norm_a, z_a)

            def modulate_before(c, par, j):
                act.wait_ge(a_full[j], A_JOBS[j] * c + 1)
                if not isinstance(c, int) or c >= 2:
                    act.wait_ge(c_full[1], C_JOBS * (c - 2) + 2)
                modulate(bank_a[j], hT[par], j, par, SA, CA).then_inc(a_free[j], 1)

            def copy_h(c, par, q):
                i, bk = q % 2, bank_a[q % 2]
                h = bk[:, :].rearrange("p (j r) -> p j r", j=2)
                pair = slice(2 * q, 2 * q + 2)
                act.wait_ge(a_full[i], A_JOBS[i] * c + 2 + q // 2)
                if not isinstance(c, int) or c >= 3:
                    act.wait_ge(result_made, c - 2)
                wait(act, tap_done, 6 * (4 * c + q - 1))
                step = 3 * (PAIRS * c + q)
                act.activation(pre[i][:, :, 0:TAPS - 1], hist[par][:, pair, :], ACT.Copy).then_inc(h_copied, 1)
                act.activation(pre[i][:, :, TAPS - 1:], h, ACT.Copy).then_inc(h_copied, 1)
                act.wait_ge(h_copied, step + 1)
                act.activation(hist[par][:, pair, :], h[:, :, ROWS - TAPS + 1:], ACT.Copy).then_inc(h_copied, 1)
                act.wait_ge(h_copied, step + 3)
                for j in range(2):
                    e = 2 * q + j
                    last = act.activation(h[:, j, :], h[:, j, :], ACT.Identity,
                                          bias=conv[:, e, TAPS:TAPS + 1], scale=conv[:, e, TAPS - 1:TAPS])
                last.then_inc(pre_made, 1)

            def tanh_before(c, q):
                act.wait_ge(tap_done, 6 * (4 * c + q + 1))
                if q == 0 and (not isinstance(c, int) or c >= 2):
                    act.wait_ge(c_free[1], C_JOBS * (c - 2) + 2)
                if q:
                    act.wait_ge(a_free[(q - 1) % 2], A_JOBS[(q - 1) % 2] * c + 2 + (q - 1) // 2)
                act.activation(tanh_s[:, :], bank_a[q % 2][:, :], ACT.Tanh).then_inc(tanh_h_made, 1)

            def skip(c, q):
                act.wait_ge(a_free[q % 2], A_JOBS[q % 2] * c + 2 + q // 2)
                if not isinstance(c, int) or c >= 2:
                    if q < PAIRS - 1:
                        act.wait_ge(pair_read, (PAIRS - 1) * (c - 2) + q + 1)
                    else:
                        act.wait_ge(c_full[1], C_JOBS * (c - 2) + 5)
                if isinstance(c, int) and c == 1:
                    act.wait_ge(stage_used[1], len(STAGED) // 2)
                for e in (2 * q, 2 * q + 1):
                    last = act.activation(yg[:, e, :], hc[:, e, :], ACT.Identity, scale=ch[:, e, SKIP:SKIP + 1])
                last.then_inc(skip_made, 1)

            def copy_dt(c):
                act.wait_ge(a_full[0], A_JOBS[0] * c + 4)
                act.activation(dtr[:, :], bank_a[0][:, 0:ROWS], ACT.Copy).then_inc(a_free[0], 1)

            def copy_b_c(c):
                act.wait_ge(a_full[1], A_JOBS[1] * c + 4)
                wait(act, b_stored, 16 * c)
                act.activation(bc_s[:, :], bank_a[1][0:2 * N, 0:ROWS], ACT.Copy).then_inc(a_free[1], 1)

            def copy_c(c, par):
                act.wait_ge(a_full[1], A_JOBS[1] * c + 7)
                if not isinstance(c, int) or c >= 2:
                    act.wait_ge(summed, STEPS * (c - 1))
                turned_bc = bank_a[1][:, 0:LB * 2 * N].rearrange("p (t n) -> p t n", t=LB)
                act.activation(c_rows[par][:, :, :], turned_bc[:, :, N:], ACT.Copy).then_inc(a_free[1], 1)

            def split_dt(c, par, q):
                act.wait_ge(a_full[q % 2], A_JOBS[q % 2] * c + 5 + q // 2)
                if not isinstance(c, int) or c >= 2:
                    act.wait_ge(ub_made, STEPS * (c - 1))
                for j in range(2):
                    e, src = 2 * q + j, bank_a[q % 2][:, j * ROWS:(j + 1) * ROWS]
                    act.activation(dt[par][:, e, :], src, ACT.Relu, bias=ch[:, e, DT_B:DT_B + 1])
                    last = act.activation(u[par][:, e, :], src, ACT.Abs, bias=ch[:, e, DT_B:DT_B + 1])
                last.then_inc(a_free[q % 2], 1)

            def soft_exps(c, par):
                act.wait_ge(a_free[0], A_JOBS[0] * c + 6)
                act.wait_ge(a_free[1], A_JOBS[1] * c + 6)
                act.activation(u[par][:, :, :], u[par][:, :, :], ACT.Exp, scale=-1.0).then_inc(soft_exp, 1)

            def soft_logs(c, par):
                act.wait_ge(soft_exp, c + 1)
                for h in range(2):
                    k = slice(h * KE // 2, (h + 1) * KE // 2)
                    act.activation(u[par][:, k, :], u[par][:, k, :], ACT.Ln, bias=1.0).then_inc(soft_ln, 1)

            def seam_decays(c, par):
                act.wait_ge(dt_made, 2 * c + 2)
                wait(act, ub_made, STEPS * (c - 1))
                for q in range(PAIRS):
                    e = 2 * q + 1
                    last = act.activation(seam[par][:, :, q], decay_rate[:, e, :], ACT.Exp, scale=dt[par][:, e, 0:1])
                last.then_inc(seam_decay, 1)

            def start_acc(c, par, j):
                t, eh = j // 2, j % 2
                act.wait_ge(a_full[j % 2], A_JOBS[j % 2] * c + 7 + j % 2 + j // 2)
                if isinstance(c, int) and c == 1:
                    act.wait_ge(stage_used[0], (len(STAGED) + 1) // 2)
                act.activation(acc[par][:, t, eh * HALF:(eh + 1) * HALF], bank_a[j % 2][:, :],
                               ACT.Copy).then_inc(a_free[j % 2], 1)

            def tanh_gate(c, q):
                act.wait_ge(c_full[q % 2], C_JOBS * c + q // 2 + 1)
                if q == 0:
                    prepared = min(c + 1, CHUNKS - 1) if isinstance(c, int) else c + 1
                    act.wait_ge(b_stored, 16 * (prepared + 1))
                    act.wait_ge(a_full[1], A_JOBS[1] * prepared + 7)
                if q:
                    act.wait_ge(c_free[(q - 1) % 2], C_JOBS * c + (q - 1) // 2 + 1)
                act.activation(tanh_s[:, :], bank_c[q % 2][:, :], ACT.Tanh, scale=0.5).then_inc(tanh_g_made, 1)

            def z_after(c):
                if not isinstance(c, int) or c + 2 < CHUNKS:
                    act.wait_ge(tap_done, 6 * PAIRS * (c + 3))
                normalize(c, nrm_c, xc, z2, norm_c, z_c)

            def modulate_after(c, par, j):
                act.wait_ge(c_full[j], C_JOBS * c + 6)
                if j == 0 and not (isinstance(c, int) and c >= CHUNKS - 2):
                    act.wait_ge(a_full[0], A_JOBS[0] * (c + 2) + 1)
                    act.wait_ge(a_full[1], A_JOBS[1] * (c + 2) + 1)
                modulate(bank_c[j], h2T, j, par, SB, CB).then_inc(c_free[j], 1)

            def rows_absolute(i):
                act.wait_ge(stage_used[i], 2)
                wait(act, rows_made, BATCH * i)
                for b in range(BATCH):
                    last = act.activation(xc[:, b, :], bank_c[b][:, :], ACT.Abs)
                last.then_inc(rows_abs, 1)

            act.wait_ge(small_loaded, 32)
            act.activation(decay_rate[:, :, :], ch[:, :, A_AT:], ACT.Exp).then_inc(rate_exp, 1)
            act.activation(cond_s[:, :, :], cond[:, :, :], ACT.Tanh, scale=0.5).then_inc(cond_tanh, 1)

            z_before(0)
            act.wait_ge(mods_made, 2)
            act.wait_ge(prep, 3)
            act.wait_ge(consts_made, 3)
            modulate_before(0, 0, 0)
            modulate_before(0, 0, 1)
            for q in (0, 2):
                copy_h(0, 0, q)
                copy_h(0, 0, q + 1)
                tanh_before(0, q)
                tanh_before(0, q + 1)
            for q in range(PAIRS):
                skip(0, q)
            copy_dt(0)
            copy_b_c(0)
            for q in range(PAIRS):
                split_dt(0, 0, q)
            soft_exps(0, 0)
            soft_logs(0, 0)
            copy_c(0, 0)
            for j in range(2 * LB):
                start_acc(0, 0, j)
            act.wait_ge(prep, 5)
            seam_decays(0, 0)

            def one_round(c, par, la, lc):
                first = isinstance(c, int) and c == 0
                for s in range(STEPS):
                    decays(c, par, 2 * s)
                    decays(c, par, 2 * s + 1)
                    if s:
                        keep_carry(c, par, s - 1)
                    elif not first:
                        keep_carry(c - 1, 1 - par, STEPS - 1)
                    if first and s in (3, 7):
                        rows_absolute(s // 4)
                    if la is not None:
                        if s == 3:
                            z_before(c + 1)
                        if s == 5:
                            modulate_before(c + 1, 1 - par, 0)
                            modulate_before(c + 1, 1 - par, 1)
                        if s in (8, 10, 13, 15):
                            copy_h(c + 1, 1 - par, {8: 0, 10: 1, 13: 2, 15: 3}[s])
                        if s in (9, 11, 14, 16):
                            tanh_before(c + 1, {9: 0, 11: 1, 14: 2, 16: 3}[s])
                        if s in (17, 18):
                            skip(c + 1, 2 * (s - 17))
                            skip(c + 1, 2 * (s - 17) + 1)
                        if s == 19:
                            copy_dt(c + 1)
                        if s == 20:
                            copy_b_c(c + 1)
                        if 22 <= s <= 25:
                            split_dt(c + 1, 1 - par, s - 22)
                        if s == 26:
                            soft_exps(c + 1, 1 - par)
                        if s == 27:
                            copy_c(c + 1, 1 - par)
                            soft_logs(c + 1, 1 - par)
                        if s == 28:
                            start_acc(c + 1, 1 - par, 0)
                        if s in (29, 30):
                            start_acc(c + 1, 1 - par, s - 28)
                        if s == 31:
                            start_acc(c + 1, 1 - par, 3)
                            seam_decays(c + 1, 1 - par)
                    if lc is not None:
                        if s in (0, 2, 4):
                            tanh_gate(c - 1, {0: 1, 2: 2, 4: 3}[s])
                        if s == 19:
                            z_after(c - 1)
                        if s == 21:
                            act.wait_ge(mods_made, 4)
                            modulate_after(c - 1, 1 - par, 0)
                            modulate_after(c - 1, 1 - par, 1)
                    if s == 29:
                        tanh_gate(c, 0)

            rounds(act, one_round)
            last = CHUNKS - 1
            for q in range(1, PAIRS):
                tanh_gate(last, q)
            z_after(last)
            modulate_after(last, 1, 0)
            modulate_after(last, 1, 1)

        @block.tensor
        def _(pe):
            def turn_states(c, g):
                s, q = g // 2, g % 2
                pe.wait_ge(scanned, UNITS * c + g + 1)
                if q == 0:
                    wait(pe, summed, STEPS * c + s)
                for j in range(2):
                    for t in range(LB):
                        at = (2 * q + j) * P
                        last = pe.transpose(turn[t][:, at:at + P], state[:, g % RING, j, t * P:(t + 1) * P], ident[:, :])
                last.then_inc(turned, 1)

            def turn_x(c, j):
                pe.wait_ge(z_a, c + 1)
                wait(pe, a_free[j], A_JOBS[j] * c)
                for i in range(2):
                    for t in range(LB):
                        k = 2 * j + i
                        last = pe.transpose(bank_a[j][:, i * ROWS + t * P:i * ROWS + (t + 1) * P],
                                            xa[:, t, k * P:(k + 1) * P], ident[:, :])
                last.then_inc(a_full[j], 1)

            def project_in(dst, full, hTc, m0, q, j):
                m = m0 + 2 * q + j
                for k in range(KD):
                    last = pe.matmul(dst[:, j * ROWS:(j + 1) * ROWS], win[:, k, m * P:(m + 1) * P], hTc[:, k, :],
                                     start=(k == 0), stop=(k == KD - 1))
                if j == 1:
                    last.then_inc(full, 1)

            def project_h(c, par, q, j):
                if j == 0:
                    pe.wait_ge(a_free[q % 2], A_JOBS[q % 2] * c + 1 + q // 2)
                    if q == 0:
                        pe.wait_ge(a_free[1], A_JOBS[1] * c + 1)
                project_in(bank_a[q % 2], a_full[q % 2], hT[par], 0, q, j)

            def project_dt(c, q):
                if q == 0:
                    pe.wait_ge(a_free[0], A_JOBS[0] * c + 3)
                    pe.wait_ge(a_free[1], A_JOBS[1] * c + 2)
                if q == PAIRS - 1:
                    pe.wait_ge(a_free[1], A_JOBS[1] * c + 3)
                for k in (2 * q, 2 * q + 1):
                    last = pe.matmul(bank_a[0][:, 0:ROWS], xp[:, k, 0:RANK_DT], hc[:, k, :], start=(k == 0), stop=(k == KE - 1))
                if q == PAIRS - 1:
                    last.then_inc(a_full[0], 1)

            def project_b_c(c, q):
                for k in (2 * q, 2 * q + 1):
                    last = pe.matmul(bank_a[1][0:2 * N, 0:ROWS], xp[:, k, RANK_DT:], hc[:, k, :],
                                     start=(k == 0), stop=(k == KE - 1))
                if q == PAIRS - 1:
                    last.then_inc(a_full[1], 1)

            def turn_b_c(c):
                for t in range(LB):
                    last = pe.transpose(bank_a[1][:, t * 2 * N:(t + 1) * 2 * N], bc_s[:, t * P:(t + 1) * P],
                                        ident[0:2 * N, 0:2 * N])
                last.then_inc(a_full[1], 1)

            def expand_dt(c, q):
                pe.wait_ge(a_free[q % 2], A_JOBS[q % 2] * c + 4 + q // 2)
                for j in range(2):
                    m = 2 * q + j
                    last = pe.matmul(bank_a[q % 2][:, j * ROWS:(j + 1) * ROWS], dtw[:, m * P:(m + 1) * P], dtr[:, :],
                                     start=True, stop=True)
                last.then_inc(a_full[q % 2], 1)

            def turn_skip(c, j):
                t, eh = j // 2, j % 2
                if j == 0:
                    pe.wait_ge(a_free[1], A_JOBS[1] * c + 6)
                pe.wait_ge(skip_made, PAIRS * c + 2 * eh + 2)
                pe.wait_ge(a_free[j % 2], A_JOBS[j % 2] * c + 6 + j % 2 + j // 2)
                for i in range(4):
                    last = pe.transpose(bank_a[j % 2][:, i * P:(i + 1) * P], yg[:, 4 * eh + i, t * P:(t + 1) * P],
                                        ident[:, :])
                last.then_inc(a_full[j % 2], 1)

            def project_gate(c, par, q, j):
                if j == 0:
                    wait(pe, c_free[q % 2], C_JOBS * c + q // 2)
                project_in(bank_c[q % 2], c_full[q % 2], hT[par], KE, q, j)

            def turn_sums(c, par, q):
                if q == 0:
                    pe.wait_ge(summed, STEPS * (c + 1))
                pe.wait_ge(c_free[q % 2], C_JOBS * c + 2 + q // 2)
                for j in range(2):
                    for t in range(LB):
                        m = 2 * q + j
                        last = pe.transpose(bank_c[q % 2][:, j * ROWS + t * P:j * ROWS + (t + 1) * P],
                                            acc[par][:, t, m * P:(m + 1) * P], ident[:, :])
                last.then_inc(c_full[q % 2], 1)

            def project_out(c, t, q):
                if q == 0:
                    pe.wait_ge(c_free[t], C_JOBS * c + 4)
                pe.wait_ge(c_free[q % 2], C_JOBS * c + 3 + q // 2)
                for k in (2 * q, 2 * q + 1):
                    last = pe.matmul(bank_c[t][:, :], yg[:, k, t * P:(t + 1) * P], wo[:, k, :],
                                     start=(k == 0), stop=(k == KE - 1))
                if t == LB - 1 and q < PAIRS - 1:
                    last.then_inc(pair_read, 1)
                if q == PAIRS - 1:
                    last.then_inc(c_full[t], 1)

            def turn_z(c, j):
                pe.wait_ge(z_c, c + 1)
                pe.wait_ge(c_free[j], C_JOBS * c + 5)
                for i in range(2):
                    for t in range(LB):
                        k = 2 * j + i
                        last = pe.transpose(bank_c[j][:, i * ROWS + t * P:i * ROWS + (t + 1) * P],
                                            z2[:, t, k * P:(k + 1) * P], ident[:, :])
                last.then_inc(c_full[j], 1)

            def ffn_bias(c, t):
                pe.wait_ge(c_free[0], C_JOBS * c + 6)
                pe.wait_ge(c_free[1], C_JOBS * c + 6)
                pe.matmul(bank_c[t][:, :], ones_row[:, :], bias_row[:, :], start=True, stop=False)

            def project_ffn(c, t, ks):
                for k in ks:
                    last = pe.matmul(bank_c[t][:, :], h2T[:, k, t * P:(t + 1) * P], ffn[:, k, :],
                                     start=False, stop=(k == KD - 1))
                if k == KD - 1:
                    last.then_inc(c_full[t], 1)

            def mod_columns(j):
                pe.wait_ge(stage_loaded[j % 2], 16 * (j // 2 + 1))
                if j in (1, 5):
                    pe.wait_ge(mods_made, j // 4 * 2 + 1)
                if j == 4:
                    pe.wait_ge(rows_made, 2 * BATCH)
                for m in range(KD):
                    for k in range(KD):
                        last = pe.matmul(bank_c[0][:, m * BATCH:(m + 1) * BATCH], staged[j % 2][:, k, m * P:(m + 1) * P],
                                         cond_h[:, k, :], start=(k == 0), stop=(k == KD - 1))
                last.then_inc(stage_used[j % 2], 1)

            def mod_rows(j, b):
                pe.wait_ge(stage_loaded[j % 2], 16 * (j // 2 + 1))
                if j == 2:
                    pe.wait_ge(mods_made, 2)
                    pe.wait_ge(prep, 4)
                wait(pe, rows_made, BATCH * (j - 2))
                for k in range(KD):
                    last = pe.matmul(bank_c[b][:, :], cond_all[:, k, b, :], staged[j % 2][:, k, :],
                                     start=(k == 0), stop=(k == KD - 1))
                if b == BATCH - 1:
                    last.then_inc(stage_used[j % 2], 1)

            pe.wait_ge(prep, 2)
            mod_columns(0)
            mod_columns(1)
            pe.wait_ge(consts_made, 3)
            turn_x(0, 0)
            turn_x(0, 1)
            pe.wait_ge(win_h_loaded, 16)
            for q in range(PAIRS):
                project_h(0, 0, q, 0)
                project_h(0, 0, q, 1)
            pe.wait_ge(xp_loaded, 32)
            for q in range(PAIRS):
                project_dt(0, q)
            for q in range(PAIRS):
                project_b_c(0, q)
            for q in range(PAIRS):
                expand_dt(0, q)
            turn_skip(0, 0)
            turn_b_c(0)
            for j in range(1, 2 * LB):
                turn_skip(0, j)

            def one_round(c, par, la, lc):
                first = isinstance(c, int) and c == 0
                for s in range(STEPS):
                    turn_states(c, 2 * s)
                    turn_states(c, 2 * s + 1)
                    if first:
                        if s in (0, 1, 4, 5):
                            mod_rows(2 + s // 4, s % 4)
                        if s in (8, 10):
                            mod_columns(s // 2)
                        if s == 26:
                            pe.wait_ge(mods_made, 4)
                            pe.wait_ge(rows_made, 2 * BATCH)
                            pe.wait_ge(late_loaded, 64)
                            pe.wait_ge(bias_scaled, 1)
                            pe.wait_ge(stage_used[0], (len(STAGED) + 1) // 2)
                    if la is not None:
                        if s == 3:
                            turn_x(c + 1, 0)
                            turn_x(c + 1, 1)
                        if 10 <= s <= 13:
                            project_h(c + 1, 1 - par, (s - 6) // 2, s % 2)
                        if s == 15:
                            project_dt(c + 1, 0)
                            project_dt(c + 1, 1)
                        if s == 17:
                            project_dt(c + 1, 2)
                            project_dt(c + 1, 3)
                        if s in (17, 18):
                            project_b_c(c + 1, 2 * (s - 17))
                            project_b_c(c + 1, 2 * (s - 17) + 1)
                        if s in (20, 22, 23):
                            expand_dt(c + 1, {20: 1, 22: 2, 23: 3}[s])
                        if s == 25:
                            turn_skip(c + 1, 0)
                            turn_b_c(c + 1)
                        if s in (27, 28):
                            turn_skip(c + 1, s - 26)
                        if s == 29:
                            turn_skip(c + 1, 3)
                    if lc is not None:
                        if 0 <= s <= 2:
                            project_gate(c - 1, 1 - par, (s + 5) // 2, (s + 1) % 2)
                        if 4 <= s <= 7:
                            turn_sums(c - 1, 1 - par, s - 4)
                    if la is not None and 5 <= s <= 8:
                        project_h(c + 1, 1 - par, (s - 5) // 2, (s - 5) % 2)
                    if lc is not None:
                        if 8 <= s <= 10:
                            project_out(c - 1, 0, s - 8)
                        if s == 13:
                            project_out(c - 1, 0, 3)
                        if s in (14, 15):
                            project_out(c - 1, 1, s - 14)
                        if s == 15:
                            project_out(c - 1, 1, 2)
                        if s == 16:
                            project_out(c - 1, 1, 3)
                        if s == 19:
                            turn_z(c - 1, 0)
                            turn_z(c - 1, 1)
                        if s == 21:
                            ffn_bias(c - 1, 0)
                            project_ffn(c - 1, 0, (0,))
                        if s == 22:
                            project_ffn(c - 1, 0, (1, 2))
                        if s == 23:
                            project_ffn(c - 1, 0, (3,))
                        if s == 24:
                            ffn_bias(c - 1, 1)
                            project_ffn(c - 1, 1, (0,))
                        if s == 25:
                            project_ffn(c - 1, 1, (1,))
                        if s == 26:
                            project_ffn(c - 1, 1, (2, 3))
                    if s in (26, 27, 28, 30):
                        project_gate(c, par, s // 28, {26: 0, 27: 1, 28: 0, 30: 1}[s])
                    if s == 31:
                        project_gate(c, par, 2, 0)
                        if la is None:
                            project_gate(c, par, 2, 1)
                    if la is not None and s == 19:
                        expand_dt(c + 1, 0)

            rounds(pe, one_round)
            last = CHUNKS - 1
            project_gate(last, 1, 3, 0)
            project_gate(last, 1, 3, 1)
            for q in range(PAIRS):
                turn_sums(last, 1, q)
            for t in range(LB):
                for q in range(PAIRS):
                    project_out(last, t, q)
            turn_z(last, 0)
            turn_z(last, 1)
            for t in range(LB):
                ffn_bias(last, t)
                project_ffn(last, t, range(KD))

        @block.vector
        def _(dve):
            def scan(c, par, g):
                n, q = g // PAIRS, g % PAIRS
                dve.wait_ge(decay_made, UNITS * c + g + 1)
                if g % 2 == 0:
                    dve.wait_ge(ub_made, STEPS * c + g // 2 + 1)
                wait(dve, turned, UNITS * c + g - RING + 1)
                wait(dve, carried, STEPS * c + (g - RING) // 2 + 1)
                dve.tensor_tensor_scan(state[:, g % RING, :, :].rearrange("p j r -> p (j r)"), decay[g % 2][:, :],
                                       ub[:, g % UB_RING, :, :].rearrange("p j r -> p (j r)"),
                                       carry[par][:, n, 2 * q:2 * q + 1], ALU.mult, ALU.add).then_inc(scanned, 1)

            def add_states(c, par, s):
                n, eh = s // 2, s % 2
                if s == 0:
                    dve.wait_ge(a_free[0], A_JOBS[0] * (c + 1))
                    dve.wait_ge(a_free[1], A_JOBS[1] * (c + 1))
                dve.wait_ge(turned, UNITS * c + 2 * s + 2)
                wait(dve, summed, STEPS * c + s - 1)
                for t in range(LB):
                    part = acc[par][:, t, eh * HALF:(eh + 1) * HALF]
                    last = dve.scalar_tensor_tensor(out=part, in0=turn[t][:, :], scalar=c_rows[par][:, t, n:n + 1],
                                                    in1=part, op0=ALU.mult, op1=ALU.add)
                last.then_inc(summed, 1)

            def stats(c, src, stat, bn, used):
                wait(dve, used, 4 * c)
                for t in range(LB):
                    last = dve.bn_stats(stat[:, t, :], src[:, t, :])
                last.then_inc(bn, 1)

            def means(stat, mv, done):
                for t in range(LB):
                    last = dve.bn_aggr(mv[:, t, :], stat[:, t, :])
                last.then_inc(done, 1)

            def stats_before(c):
                dve.wait_ge(xa_loaded, 16 * c + 16)
                stats(c, xa, stat_a, bn_a, norm_a)

            def taps(c, q):
                bk = bank_a[q % 2]
                dve.wait_ge(pre_made, PAIRS * c + q + 1)
                for k in range(TAPS - 1):
                    for j in range(2):
                        e, part = 2 * q + j, bk[:, j * ROWS:(j + 1) * ROWS]
                        if k:
                            dve.wait_ge(tap_done, 6 * (4 * c + q) + 2 * (k - 1) + j + 1)
                        dve.scalar_tensor_tensor(out=part, in0=pre[q % 2][:, j, k:k + ROWS], scalar=conv[:, e, k:k + 1],
                                                 in1=part, op0=ALU.mult, op1=ALU.add).then_inc(tap_done, 1)

            def silu_before(c, q):
                dve.wait_ge(tanh_h_made, PAIRS * c + q + 1)
                if q == 0:
                    wait(dve, u_made, 2 * c)
                    wait(dve, skip_made, PAIRS * c)
                dve.scalar_tensor_tensor(out=hc[:, 2 * q:2 * q + 2, :].rearrange("p k r -> p (k r)"), in0=tanh_s[:, :],
                                         scalar=1.0, in1=bank_a[q % 2][:, :], op0=ALU.add,
                                         op1=ALU.mult).then_inc(a_free[q % 2], 1)

            def add_dt(c, par, h):
                k = slice(h * KE // 2, (h + 1) * KE // 2)
                dve.wait_ge(soft_ln, 2 * c + h + 1)
                dve.tensor_tensor(dt[par][:, k, :], dt[par][:, k, :], u[par][:, k, :], ALU.add).then_inc(dt_made, 1)

            def silu_gate(c, q):
                if q == 0:
                    done = min(c + 2, CHUNKS) if isinstance(c, int) else c + 2
                    dve.wait_ge(a_full[0], A_JOBS[0] * done)
                    dve.wait_ge(a_full[1], A_JOBS[1] * done)
                dve.wait_ge(tanh_g_made, PAIRS * c + q + 1)
                dve.scalar_tensor_tensor(out=yg[:, 2 * q:2 * q + 2, :].rearrange("p k r -> p (k r)"), in0=tanh_s[:, :],
                                         scalar=1.0, in1=bank_c[q % 2][:, :], op0=ALU.add,
                                         op1=ALU.mult).then_inc(c_free[q % 2], 1)

            def gate_sums(c, q):
                dve.wait_ge(c_full[q % 2], C_JOBS * c + 3 + q // 2)
                part = yg[:, 2 * q:2 * q + 2, :].rearrange("p k r -> p (k r)")
                dve.tensor_tensor(part, bank_c[q % 2][:, :], part, ALU.mult).then_inc(c_free[q % 2], 1)

            def residual_mixer(c, par, t):
                if t == 0:
                    dve.wait_ge(xc_loaded, 16 * c + 16)
                dve.wait_ge(c_full[t], C_JOBS * c + 5)
                dve.tensor_tensor(bank_c[t][:, :], bank_c[t][:, :], ga[:, par, :], ALU.mult).then_inc(o_scaled, 1)
                dve.wait_ge(o_scaled, LB * c + t + 1)
                dve.tensor_tensor(xc[:, t, :], bank_c[t][:, :], xc[:, t, :], ALU.add).then_inc(c_free[t], 1)

            def stats_after(c):
                dve.wait_ge(c_free[0], C_JOBS * c + 5)
                dve.wait_ge(c_free[1], C_JOBS * c + 5)
                stats(c, xc, stat_c, bn_c, norm_c)

            def scale_ffn(c, par, t):
                dve.wait_ge(c_full[t], C_JOBS * c + 7)
                dve.tensor_tensor(z2[:, t, :], bank_c[t][:, :], gb[:, par, :], ALU.mult).then_inc(c_free[t], 1)

            def copy_mods(j, kind):
                dve.wait_ge(stage_used[j % 2], j // 2 + 1)
                dst = mods[:, kind, :, :].rearrange("p k b -> p (k b)")
                one = 1.0 if kind in (CA, CB) else 0.0
                dve.tensor_scalar(dst, bank_c[0][:, 0:KD * BATCH], one, None, ALU.add).then_inc(mods_made, 1)

            def clamp_rows(i, gates, factor):
                dve.wait_ge(rows_abs, i + 1)
                for b in range(BATCH):
                    n = 2 * BATCH * i + 2 * b
                    g = gates[:, b, :]
                    dve.tensor_scalar(g, bank_c[b][:, :], 0.0, 2.0 * factor, ALU.is_ge, ALU.mult).then_inc(rows_sign, 1)
                    dve.wait_ge(rows_sign, n + 1)
                    dve.tensor_scalar(g, g, -factor, None, ALU.add).then_inc(rows_sign, 1)
                    dve.wait_ge(rows_sign, n + 2)
                    dve.scalar_tensor_tensor(out=g, in0=xc[:, b, :], scalar=0.25, in1=g, op0=ALU.max,
                                             op1=ALU.mult).then_inc(rows_made, 1)

            def add_factor(j):
                dve.wait_ge(stage_loaded[j % 2], 16 * (j // 2 + 1))
                if j > MODS:
                    dve.wait_ge(stage_used[(j - 1) % 2], (j - 1) // 2 + 1)
                dve.tensor_tensor(ffn[:, :, :], ffn[:, :, :], staged[j % 2], ALU.add).then_inc(stage_used[j % 2], 1)

            dve.wait_ge(cond_tanh, 1)
            dve.scalar_tensor_tensor(out=cond_s[:, :, :], in0=cond_s[:, :, :], scalar=1.0, in1=cond[:, :, :],
                                     op0=ALU.add, op1=ALU.mult).then_inc(prep, 1)
            dve.wait_ge(prep, 1)
            dve.tensor_scalar(cond_h[:, :, :], cond_s[:, :, :], 0.5, None, ALU.mult).then_inc(prep, 1)
            dve.tensor_scalar(conv[:, :, :], ch[:, :, 0:TAPS + 1], 0.5, None, ALU.mult).then_inc(prep, 1)
            stats_before(0)
            dve.wait_ge(bn_a, 1)
            means(stat_a, mv_a, stats_a)
            copy_mods(0, SA)
            copy_mods(1, CA)
            dve.wait_ge(prep, 2)
            dve.tensor_copy(cond_all, cond_h[:, :, :].unsqueeze(3).to_broadcast([P, KD, BATCH, P])).then_inc(prep, 1)
            dve.wait_ge(rate_exp, 1)
            dve.tensor_scalar(decay_rate[:, :, :], decay_rate[:, :, :], -1.0, None, ALU.mult).then_inc(prep, 1)
            for i in range(2):
                last = dve.memset(decay[i][:, ROWS:ROWS + 1], 0.0)
            last.then_inc(seam_zeroed, 1)
            for q in (0, 2):
                taps(0, q)
                taps(0, q + 1)
                silu_before(0, q)
                silu_before(0, q + 1)
            add_dt(0, 0, 0)
            add_dt(0, 0, 1)
            dve.wait_ge(seam_zeroed, 1)

            def one_round(c, par, la, lc):
                first = isinstance(c, int) and c == 0
                for s in range(STEPS):
                    if la is not None and s == 2:
                        dve.wait_ge(bn_a, c + 2)
                    if lc is not None and s == 18:
                        dve.wait_ge(bn_c, c)
                    scan(c, par, 2 * s)
                    if la is not None and s == 2:
                        means(stat_a, mv_a, stats_a)
                    if lc is not None and s == 18:
                        means(stat_c, mv_c, stats_c)
                    scan(c, par, 2 * s + 1)
                    if s:
                        add_states(c, par, s - 1)
                    elif not first:
                        add_states(c - 1, 1 - par, STEPS - 1)
                    if first:
                        if s in (3, 7):
                            clamp_rows(s // 4, *[(ga, 0.5), (gb, RANK ** -0.5)][s // 4])
                        if s in (9, 11):
                            copy_mods(s // 2, (SB, CB)[s // 11])
                        if MODS + 5 <= s < MODS + 4 + RANK:
                            add_factor(s - 5)
                        if s == MODS + 4 + RANK:
                            dve.wait_ge(late_loaded, 64)
                            dve.tensor_scalar(bias_row[:, :], bias_row[:, :], math.sqrt(RANK), None,
                                              ALU.mult).then_inc(bias_scaled, 1)
                    if lc is not None:
                        if s in (0, 2, 4):
                            silu_gate(c - 1, {0: 1, 2: 2, 4: 3}[s])
                        if 5 <= s <= 8:
                            gate_sums(c - 1, s - 5)
                        if s in (15, 17):
                            residual_mixer(c - 1, 1 - par, s // 17)
                        if s == 17:
                            stats_after(c - 1)
                        if s in (25, 27):
                            scale_ffn(c - 1, 1 - par, s // 27)
                    if la is not None:
                        if s == 1:
                            stats_before(c + 1)
                        if s in (8, 10, 13, 15):
                            taps(c + 1, {8: 0, 10: 1, 13: 2, 15: 3}[s])
                        if s in (9, 11, 14, 16):
                            silu_before(c + 1, {9: 0, 11: 1, 14: 2, 16: 3}[s])
                        if s == 28:
                            add_dt(c + 1, 1 - par, 0)
                            add_dt(c + 1, 1 - par, 1)
                    if s == 30:
                        silu_gate(c, 0)

            rounds(dve, one_round)
            last = CHUNKS - 1
            add_states(last, 1, STEPS - 1)
            for q in range(1, PAIRS):
                silu_gate(last, q)
            for q in range(PAIRS):
                gate_sums(last, q)
            residual_mixer(last, 1, 0)
            residual_mixer(last, 1, 1)
            stats_after(last)
            dve.wait_ge(bn_c, CHUNKS)
            means(stat_c, mv_c, stats_c)
            scale_ffn(last, 1, 0)
            scale_ffn(last, 1, 1)


def kernel(**inputs):
    import numpy as np
    import concourse.bacc as bacc
    from concourse.bass_utils import run_bass_kernel_spmd

    def tiles(a):
        a = np.asarray(a)
        return a.reshape(a.shape[0] // P, P, -1).transpose(1, 0, 2)

    at = {k.removeprefix("L0_"): np.asarray(v) for k, v in inputs.items()}
    chan = np.concatenate([tiles(at[k]) for k in ("attn_conv_w", "attn_conv_b", "attn_dt_proj_b", "attn_D", "attn_A_log")], axis=2)
    arrays = {
        "x": at["attn_hidden_states"], "win_t": at["attn_in_proj_w"].T, "xp_t": at["attn_x_proj_w"].T,
        "dt_t": at["attn_dt_proj_w"].T, "wo_t": at["attn_out_proj_w"].T, "chan": chan,
        "cond_t": tiles(at["c"].T), "wmod": at["wmod"], "factors": at["ffn_factors"], "bias": at["ffn_bias"],
    }
    arrays = {k: np.ascontiguousarray(v) for k, v in arrays.items()}
    nc = bacc.Bacc("TRN2", target_bir_lowering=False, num_devices=1)
    args = [nc.dram_tensor(k, v.shape, mybir.dt.from_np(v.dtype), kind="ExternalInput").ap() for k, v in arrays.items()]
    out = nc.dram_tensor("out", (BATCH, SEQ, DIM), F32, kind="ExternalOutput").ap()
    build(nc, *args, out)
    r = run_bass_kernel_spmd(nc, [arrays], core_ids=[0])
    return r.results[0]["out"]
```
